# Optimizing a Trainium2 kernel written in Bass

```python
import numpy as np
import jax
import jax.numpy as jnp

def _softmax(x, axis=-1):
    return jax.nn.softmax(x, axis=axis)

def _gelu(x):
    return jax.nn.gelu(x, approximate=True)

def _silu(x):
    return jax.nn.silu(x)

def _sigmoid(x):
    return jax.nn.sigmoid(x)

def _layernorm(x, axis=-1, eps=1e-05):
    m = jnp.mean(x, axis=axis, keepdims=True)
    v = jnp.var(x, axis=axis, keepdims=True)
    return (x - m) / jnp.sqrt(v + eps)

def _scatter_add(tgt, idx, src, axis=0):
    return tgt.at[idx].add(src)

def _segment_sum(src, seg, n):
    return jax.ops.segment_sum(src, seg, n)
kernel_name = 'mk_prb_d2_jaxref_r8_c8ced8'

def setup_inputs(seed: int=0):
    np.random.seed(seed)
    _w = jnp.asarray

    def _L0_attn_setup():
        import jax, jax.numpy as jnp
        import numpy as np
        D_MODEL = 256
        N_HEAD = 16
        MLP_HIDDEN = 704
        NORMALIZER = 16.0

        def rmsnorm(x, w, eps=1e-05):
            return x * jax.lax.rsqrt(jnp.mean(x * x, axis=-1, keepdims=True) + eps) * w

        def _reference_tuple_inner(x, Wq, Wk, Wkg1, Wkg2, bkg2, Wv, Wg, bg, Wo, ln1_w, ln2_w, W1, W3, W2):
            B, L, d = x.shape
            H = N_HEAD
            hd = d // H
            kd = d // 2 // H
            scaling = (d // H) ** (-0.5)
            xn = rmsnorm(x, ln1_w)
            q = xn @ Wq
            k = xn @ Wk * scaling
            gk = jax.nn.log_sigmoid(xn @ Wkg1 @ Wkg2 + bkg2) / NORMALIZER
            v = xn @ Wv
            g = xn @ Wg + bg
            split = lambda t, dh: t.reshape(B, L, H, dh).transpose(1, 0, 2, 3)
            qh, kh, gh = (split(q, kd), split(k, kd), split(gk, kd))
            vh = split(v, hd)
            S0 = jnp.zeros((B, H, kd, hd), x.dtype)

            def step(S, inp):
                qt, kt, vt, gt = inp
                S = S * jnp.exp(gt)[..., None] + kt[..., None] * vt[..., None, :]
                ot = jnp.einsum('bhk,bhkd->bhd', qt, S)
                return (S, ot)
            Sf, o = jax.lax.scan(step, S0, (qh, kh, vh, gh))
            mu = jnp.mean(o, axis=-1, keepdims=True)
            var = jnp.var(o, axis=-1, keepdims=True)
            o = (o - mu) * jax.lax.rsqrt(var + 1e-05)
            o = o.transpose(1, 0, 2, 3).reshape(B, L, d)
            o = jax.nn.silu(g) * o
            x = x + o @ Wo
            xn2 = rmsnorm(x, ln2_w)
            x = x + jax.nn.silu(xn2 @ W1) * (xn2 @ W3) @ W2
            return (x, Sf)
        key = jax.random.key(seed)
        d, B, L, Hd = (D_MODEL, 2, 512, MLP_HIDDEN)
        ks = jax.random.split(key, 12)
        w = lambda k, shape, s=0.02: jax.random.normal(k, shape, jnp.float32) * s
        return {'x': jax.random.normal(ks[0], (B, L, d), jnp.float32), 'Wq': w(ks[1], (d, d // 2)), 'Wk': w(ks[2], (d, d // 2)), 'Wkg1': w(ks[3], (d, 16)), 'Wkg2': w(ks[4], (16, d // 2)), 'bkg2': jnp.zeros((d // 2,), jnp.float32), 'Wv': w(ks[5], (d, d)), 'Wg': w(ks[6], (d, d)), 'bg': jnp.zeros((d,), jnp.float32), 'Wo': w(ks[7], (d, d)), 'ln1_w': jnp.ones((d,), jnp.float32), 'ln2_w': jnp.ones((d,), jnp.float32), 'W1': w(ks[8], (d, Hd)), 'W3': w(ks[9], (d, Hd)), 'W2': w(ks[10], (Hd, d))}
    _L0_attn_in = _L0_attn_setup()

    def _L0_ffn_setup():
        import jax, jax.numpy as jnp
        import numpy as np
        GROUP_SIZE = 64

        def ternary_quant(w_fp32, g=GROUP_SIZE):
            w = w_fp32.astype(jnp.bfloat16)
            w_g = w.reshape(-1, g)
            scale = jnp.clip(jnp.mean(jnp.abs(w_g), axis=-1, keepdims=True), 1e-08, None)
            q = jnp.clip(jnp.round(w_g / scale), -1, 1)
            w_hat = (q * scale).reshape(w.shape)
            return w + jax.lax.stop_gradient(w_hat - w)

        def rms_norm(x):
            eps = jnp.finfo(x.dtype).eps.astype(jnp.float32)
            xf = x.astype(jnp.float32)
            inv = jax.lax.rsqrt(jnp.mean(xf * xf, axis=-1, keepdims=True) + eps)
            return (xf * inv).astype(x.dtype)
        key = jax.random.key(seed)
        k1, k2, k3 = jax.random.split(key, 3)
        B, S, D = (2, 256, 256)
        H = 4 * D
        x = jax.random.normal(k1, (B, S, D), dtype=jnp.float32).astype(jnp.bfloat16)
        w_gate_up = jax.random.normal(k2, (2 * H, D), dtype=jnp.float32) * 0.02
        w_proj = jax.random.normal(k3, (D, H), dtype=jnp.float32) * 0.02
        return {'x': x, 'w_gate_up': w_gate_up, 'w_proj': w_proj}
    _L0_ffn_in = _L0_ffn_setup()

    def _L1_attn_setup():
        import jax, jax.numpy as jnp
        import numpy as np
        NUM_HEADS = 16
        HIDDEN = 256
        HEAD_DIM = HIDDEN // NUM_HEADS
        ROTARY_DIM = HEAD_DIM // 4
        ROPE_BASE = 10000.0

        def _rope_angles(seq_len, dtype=jnp.float32):
            inv_freq = 1.0 / ROPE_BASE ** (jnp.arange(0, ROTARY_DIM, 2, dtype=dtype) / ROTARY_DIM)
            t = jnp.arange(seq_len, dtype=dtype)
            freqs = jnp.einsum('s,d->sd', t, inv_freq)
            emb = jnp.concatenate([freqs, freqs], axis=-1)
            return (jnp.cos(emb), jnp.sin(emb))

        def _rotate_half(x):
            x1, x2 = jnp.split(x, 2, axis=-1)
            return jnp.concatenate([-x2, x1], axis=-1)
        key = jax.random.key(seed)
        k1, k2, k3 = jax.random.split(key, 3)
        B, S = (2, 256)
        scale_qkv = 1.0 / np.sqrt(HIDDEN)
        return {'hidden_states': jax.random.normal(k1, (B, S, HIDDEN), dtype=jnp.float32), 'w_qkv': jax.random.normal(k2, (HIDDEN, 3 * HIDDEN), dtype=jnp.float32) * scale_qkv, 'b_qkv': jnp.zeros((3 * HIDDEN,), dtype=jnp.float32), 'w_out': jax.random.normal(k3, (HIDDEN, HIDDEN), dtype=jnp.float32) * scale_qkv, 'b_out': jnp.zeros((HIDDEN,), dtype=jnp.float32)}
    _L1_attn_in = _L1_attn_setup()

    def _L1_ffn_setup():
        import jax, jax.numpy as jnp
        import numpy as np
        B, S, HID = (2, 256, 256)
        NUM_HEADS = 16
        HEAD_DIM = HID // NUM_HEADS
        NUM_EXPERTS = 8
        TOP_K = 2
        INTER = 512
        EPS = 1e-05

        def _rmsnorm(x, w, eps=EPS):
            return x * jax.lax.rsqrt(jnp.mean(x * x, axis=-1, keepdims=True) + eps) * w

        def _moe(x_flat, Wr, Wg, Wu, Wd):
            T = x_flat.shape[0]
            logits = x_flat @ Wr.T
            top_logits, top_idx = jax.lax.top_k(logits, TOP_K)
            probs = jax.nn.softmax(top_logits, axis=-1)
            cw = jnp.zeros((T, NUM_EXPERTS), x_flat.dtype)
            cw = cw.at[jnp.arange(T)[:, None], top_idx].add(probs)
            hg = jnp.einsum('eih,th->eti', Wg, x_flat)
            hu = jnp.einsum('eih,th->eti', Wu, x_flat)
            y = jnp.einsum('ehi,eti->eth', Wd, jax.nn.silu(hg) * hu)
            return jnp.einsum('eth,te->th', y, cw)
        key = jax.random.key(seed)
        ks = jax.random.split(key, 12)
        sd_h = 1.0 / np.sqrt(HID)
        sd_i = 1.0 / np.sqrt(INTER)
        return {'x': jax.random.normal(ks[0], (B, S, HID), jnp.float32), 'Wq': jax.random.normal(ks[1], (HID, HID), jnp.float32) * sd_h, 'Wk': jax.random.normal(ks[2], (HID, HID), jnp.float32) * sd_h, 'Wv': jax.random.normal(ks[3], (HID, HID), jnp.float32) * sd_h, 'Wo': jax.random.normal(ks[4], (HID, HID), jnp.float32) * sd_h, 'w_ln1': jnp.ones((HID,), jnp.float32), 'w_ln2': jnp.ones((HID,), jnp.float32), 'Wr': jax.random.normal(ks[5], (NUM_EXPERTS, HID), jnp.float32) * sd_h, 'Wg': jax.random.normal(ks[6], (NUM_EXPERTS, INTER, HID), jnp.float32) * sd_h, 'Wu': jax.random.normal(ks[7], (NUM_EXPERTS, INTER, HID), jnp.float32) * sd_h, 'Wd': jax.random.normal(ks[8], (NUM_EXPERTS, HID, INTER), jnp.float32) * sd_i}
    _L1_ffn_in = _L1_ffn_setup()
    _d = {'L0_attn_x': _L0_attn_in['x'], 'L0_attn_Wq': _L0_attn_in['Wq'], 'L0_attn_Wk': _L0_attn_in['Wk'], 'L0_attn_Wkg1': _L0_attn_in['Wkg1'], 'L0_attn_Wkg2': _L0_attn_in['Wkg2'], 'L0_attn_bkg2': _L0_attn_in['bkg2'], 'L0_attn_Wv': _L0_attn_in['Wv'], 'L0_attn_Wg': _L0_attn_in['Wg'], 'L0_attn_bg': _L0_attn_in['bg'], 'L0_attn_Wo': _L0_attn_in['Wo'], 'L0_attn_ln1_w': _L0_attn_in['ln1_w'], 'L0_attn_ln2_w': _L0_attn_in['ln2_w'], 'L0_attn_W1': _L0_attn_in['W1'], 'L0_attn_W3': _L0_attn_in['W3'], 'L0_attn_W2': _L0_attn_in['W2'], 'L0_ffn_w_gate_up': _L0_ffn_in['w_gate_up'], 'L0_ffn_w_proj': _L0_ffn_in['w_proj'], 'L1_attn_w_qkv': _L1_attn_in['w_qkv'], 'L1_attn_b_qkv': _L1_attn_in['b_qkv'], 'L1_attn_w_out': _L1_attn_in['w_out'], 'L1_attn_b_out': _L1_attn_in['b_out'], 'L1_ffn_Wq': _L1_ffn_in['Wq'], 'L1_ffn_Wk': _L1_ffn_in['Wk'], 'L1_ffn_Wv': _L1_ffn_in['Wv'], 'L1_ffn_Wo': _L1_ffn_in['Wo'], 'L1_ffn_w_ln1': _L1_ffn_in['w_ln1'], 'L1_ffn_w_ln2': _L1_ffn_in['w_ln2'], 'L1_ffn_Wr': _L1_ffn_in['Wr'], 'L1_ffn_Wg': _L1_ffn_in['Wg'], 'L1_ffn_Wu': _L1_ffn_in['Wu'], 'L1_ffn_Wd': _L1_ffn_in['Wd']}
    _x0 = _d['L0_attn_x']
    _d['L0_attn_x'] = jax.random.normal(jax.random.fold_in(jax.random.key(seed), 1), (2, 512, 256), dtype=_x0.dtype)
    del _x0
    return _d

def reference(L0_attn_x, L0_attn_Wq, L0_attn_Wk, L0_attn_Wkg1, L0_attn_Wkg2, L0_attn_bkg2, L0_attn_Wv, L0_attn_Wg, L0_attn_bg, L0_attn_Wo, L0_attn_ln1_w, L0_attn_ln2_w, L0_attn_W1, L0_attn_W3, L0_attn_W2, L0_ffn_w_gate_up, L0_ffn_w_proj, L1_attn_w_qkv, L1_attn_b_qkv, L1_attn_w_out, L1_attn_b_out, L1_ffn_Wq, L1_ffn_Wk, L1_ffn_Wv, L1_ffn_Wo, L1_ffn_w_ln1, L1_ffn_w_ln2, L1_ffn_Wr, L1_ffn_Wg, L1_ffn_Wu, L1_ffn_Wd):

    def _L0_attn_ref(x, Wq, Wk, Wkg1, Wkg2, bkg2, Wv, Wg, bg, Wo, ln1_w, ln2_w, W1, W3, W2):
        import jax, jax.numpy as jnp
        import numpy as np
        D_MODEL = 256
        N_HEAD = 16
        MLP_HIDDEN = 704
        NORMALIZER = 16.0

        def rmsnorm(x, w, eps=1e-05):
            return x * jax.lax.rsqrt(jnp.mean(x * x, axis=-1, keepdims=True) + eps) * w

        def _reference_tuple_inner(x, Wq, Wk, Wkg1, Wkg2, bkg2, Wv, Wg, bg, Wo, ln1_w, ln2_w, W1, W3, W2):
            B, L, d = x.shape
            H = N_HEAD
            hd = d // H
            kd = d // 2 // H
            scaling = (d // H) ** (-0.5)
            xn = rmsnorm(x, ln1_w)
            q = xn @ Wq
            k = xn @ Wk * scaling
            gk = jax.nn.log_sigmoid(xn @ Wkg1 @ Wkg2 + bkg2) / NORMALIZER
            v = xn @ Wv
            g = xn @ Wg + bg
            split = lambda t, dh: t.reshape(B, L, H, dh).transpose(1, 0, 2, 3)
            qh, kh, gh = (split(q, kd), split(k, kd), split(gk, kd))
            vh = split(v, hd)
            S0 = jnp.zeros((B, H, kd, hd), x.dtype)

            def step(S, inp):
                qt, kt, vt, gt = inp
                S = S * jnp.exp(gt)[..., None] + kt[..., None] * vt[..., None, :]
                ot = jnp.einsum('bhk,bhkd->bhd', qt, S)
                return (S, ot)
            Sf, o = jax.lax.scan(step, S0, (qh, kh, vh, gh))
            mu = jnp.mean(o, axis=-1, keepdims=True)
            var = jnp.var(o, axis=-1, keepdims=True)
            o = (o - mu) * jax.lax.rsqrt(var + 1e-05)
            o = o.transpose(1, 0, 2, 3).reshape(B, L, d)
            o = jax.nn.silu(g) * o
            x = x + o @ Wo
            xn2 = rmsnorm(x, ln2_w)
            x = x + jax.nn.silu(xn2 @ W1) * (xn2 @ W3) @ W2
            return (x, Sf)
        return _reference_tuple_inner(x, Wq, Wk, Wkg1, Wkg2, bkg2, Wv, Wg, bg, Wo, ln1_w, ln2_w, W1, W3, W2)[0]

    def _L0_ffn_ref(x, w_gate_up, w_proj):
        import jax, jax.numpy as jnp
        import numpy as np
        GROUP_SIZE = 64

        def ternary_quant(w_fp32, g=GROUP_SIZE):
            w = w_fp32.astype(jnp.bfloat16)
            w_g = w.reshape(-1, g)
            scale = jnp.clip(jnp.mean(jnp.abs(w_g), axis=-1, keepdims=True), 1e-08, None)
            q = jnp.clip(jnp.round(w_g / scale), -1, 1)
            w_hat = (q * scale).reshape(w.shape)
            return w + jax.lax.stop_gradient(w_hat - w)

        def rms_norm(x):
            eps = jnp.finfo(x.dtype).eps.astype(jnp.float32)
            xf = x.astype(jnp.float32)
            inv = jax.lax.rsqrt(jnp.mean(xf * xf, axis=-1, keepdims=True) + eps)
            return (xf * inv).astype(x.dtype)
        wq_gu = ternary_quant(w_gate_up)
        gu = jnp.einsum('bsd,hd->bsh', x, wq_gu)
        gate, up = jnp.split(gu, 2, axis=-1)
        h = jax.nn.silu(gate) * up
        hn = rms_norm(h)
        wq_p = ternary_quant(w_proj)
        return jnp.einsum('bsh,dh->bsd', hn, wq_p)

    def _L1_attn_ref(hidden_states, w_qkv, b_qkv, w_out, b_out):
        import jax, jax.numpy as jnp
        import numpy as np
        NUM_HEADS = 16
        HIDDEN = 256
        HEAD_DIM = HIDDEN // NUM_HEADS
        ROTARY_DIM = HEAD_DIM // 4
        ROPE_BASE = 10000.0

        def _rope_angles(seq_len, dtype=jnp.float32):
            inv_freq = 1.0 / ROPE_BASE ** (jnp.arange(0, ROTARY_DIM, 2, dtype=dtype) / ROTARY_DIM)
            t = jnp.arange(seq_len, dtype=dtype)
            freqs = jnp.einsum('s,d->sd', t, inv_freq)
            emb = jnp.concatenate([freqs, freqs], axis=-1)
            return (jnp.cos(emb), jnp.sin(emb))

        def _rotate_half(x):
            x1, x2 = jnp.split(x, 2, axis=-1)
            return jnp.concatenate([-x2, x1], axis=-1)
        B, S, H = hidden_states.shape
        qkv = jnp.einsum('bsh,hf->bsf', hidden_states, w_qkv) + b_qkv
        qkv = qkv.reshape(B, S, NUM_HEADS, 3 * HEAD_DIM)
        q = jnp.transpose(qkv[..., :HEAD_DIM], (0, 2, 1, 3))
        k = jnp.transpose(qkv[..., HEAD_DIM:2 * HEAD_DIM], (0, 2, 1, 3))
        v = jnp.transpose(qkv[..., 2 * HEAD_DIM:], (0, 2, 1, 3))
        cos, sin = _rope_angles(S, q.dtype)
        q_rot, q_pass = (q[..., :ROTARY_DIM], q[..., ROTARY_DIM:])
        k_rot, k_pass = (k[..., :ROTARY_DIM], k[..., ROTARY_DIM:])
        q_rot = q_rot * cos + _rotate_half(q_rot) * sin
        k_rot = k_rot * cos + _rotate_half(k_rot) * sin
        q = jnp.concatenate([q_rot, q_pass], axis=-1)
        k = jnp.concatenate([k_rot, k_pass], axis=-1)
        scores = jnp.einsum('bhqd,bhkd->bhqk', q, k)
        causal = jnp.tril(jnp.ones((S, S), dtype=bool))
        scores = jnp.where(causal, scores, jnp.float32(-jnp.inf).astype(scores.dtype))
        probs = jax.nn.softmax(scores, axis=-1)
        attn = jnp.einsum('bhqk,bhkd->bhqd', probs, v)
        attn = jnp.transpose(attn, (0, 2, 1, 3)).reshape(B, S, H)
        return jnp.einsum('bsh,hf->bsf', attn, w_out) + b_out

    def _L1_ffn_ref(x, Wq, Wk, Wv, Wo, w_ln1, w_ln2, Wr, Wg, Wu, Wd):
        import jax, jax.numpy as jnp
        import numpy as np
        B, S, HID = (2, 256, 256)
        NUM_HEADS = 16
        HEAD_DIM = HID // NUM_HEADS
        NUM_EXPERTS = 8
        TOP_K = 2
        INTER = 512
        EPS = 1e-05

        def _rmsnorm(x, w, eps=EPS):
            return x * jax.lax.rsqrt(jnp.mean(x * x, axis=-1, keepdims=True) + eps) * w

        def _moe(x_flat, Wr, Wg, Wu, Wd):
            T = x_flat.shape[0]
            logits = x_flat @ Wr.T
            top_logits, top_idx = jax.lax.top_k(logits, TOP_K)
            probs = jax.nn.softmax(top_logits, axis=-1)
            cw = jnp.zeros((T, NUM_EXPERTS), x_flat.dtype)
            cw = cw.at[jnp.arange(T)[:, None], top_idx].add(probs)
            hg = jnp.einsum('eih,th->eti', Wg, x_flat)
            hu = jnp.einsum('eih,th->eti', Wu, x_flat)
            y = jnp.einsum('ehi,eti->eth', Wd, jax.nn.silu(hg) * hu)
            return jnp.einsum('eth,te->th', y, cw)
        b, s, hid = x.shape
        residual = x
        xn = _rmsnorm(x, w_ln1)
        q = (xn @ Wq.T).reshape(b, s, NUM_HEADS, HEAD_DIM)
        k = (xn @ Wk.T).reshape(b, s, NUM_HEADS, HEAD_DIM)
        v = (xn @ Wv.T).reshape(b, s, NUM_HEADS, HEAD_DIM)
        scale = 1.0 / np.sqrt(HEAD_DIM)
        attn = jnp.einsum('bqhd,bkhd->bhqk', q, k) * scale
        causal = jnp.tril(jnp.ones((s, s), bool))
        attn = jnp.where(causal[None, None], attn, -jnp.inf)
        attn = jax.nn.softmax(attn, axis=-1)
        h = jnp.einsum('bhqk,bkhd->bqhd', attn, v).reshape(b, s, hid)
        x = residual + h @ Wo.T
        residual = x
        xn = _rmsnorm(x, w_ln2)
        moe_out = _moe(xn.reshape(-1, hid), Wr, Wg, Wu, Wd).reshape(b, s, hid)
        return residual + moe_out
    x = L0_attn_x
    xn = _layernorm(x, axis=-1)
    x = x + _L0_attn_ref(xn, L0_attn_Wq, L0_attn_Wk, L0_attn_Wkg1, L0_attn_Wkg2, L0_attn_bkg2, L0_attn_Wv, L0_attn_Wg, L0_attn_bg, L0_attn_Wo, L0_attn_ln1_w, L0_attn_ln2_w, L0_attn_W1, L0_attn_W3, L0_attn_W2) + _L0_ffn_ref(xn, L0_ffn_w_gate_up, L0_ffn_w_proj)
    xn = _layernorm(x, axis=-1)
    x = x + _L1_attn_ref(xn, L1_attn_w_qkv, L1_attn_b_qkv, L1_attn_w_out, L1_attn_b_out) + _L1_ffn_ref(xn, L1_ffn_Wq, L1_ffn_Wk, L1_ffn_Wv, L1_ffn_Wo, L1_ffn_w_ln1, L1_ffn_w_ln2, L1_ffn_Wr, L1_ffn_Wg, L1_ffn_Wu, L1_ffn_Wd)
    return x

_drawn_inputs = setup_inputs


def setup_inputs(seed=0):
    import zlib

    import numpy as np

    out = dict(_drawn_inputs(seed))
    spreads = {'L0_attn_bkg2': (0.0, 2.0),
     'L0_attn_bg': (0.0, 0.469),
     'L0_attn_ln1_w': (1.0, 0.6),
     'L0_attn_ln2_w': (1.0, 0.6),
     'L1_attn_b_qkv': (0.0, 0.1),
     'L1_attn_b_out': (0.0, 0.1),
     'L1_ffn_w_ln1': (1.0, 0.2),
     'L1_ffn_w_ln2': (1.0, 0.2)}
    factors = {'L0_attn_Wkg1': 27.148, 'L0_attn_Wkg2': 25.456}
    for name, (base, spread) in spreads.items():
        noise = np.random.default_rng([zlib.crc32(name.encode()), seed]).standard_normal(out[name].shape)
        drawn = base * np.exp(spread * noise) if base else spread * noise
        out[name] = jnp.asarray(drawn.astype(out[name].dtype))
    for name, factor in factors.items():
        out[name] = (out[name] * factor).astype(out[name].dtype)
    return out
```

```python
import math

import numpy as np
import concourse.bass as bass
from concourse import mybir
from concourse.alu_op_type import AluOpType as ALU

F32 = mybir.dt.float32
F32R = mybir.dt.float32r
BF16 = mybir.dt.bfloat16
I32 = mybir.dt.int32
U32 = mybir.dt.uint32
ACT = mybir.ActivationFunctionType
AX = mybir.AxisListType

P = 128
D = 256
KC = D // P
CH = 512
NC = 2
TPC = CH // P
NT = NC * TPC
H = 16
HD = D // H
KD = 8
FF_STEPS = 8
SW = [128, 128, 128, 128, 96, 96]
SWO = [sum(SW[:i]) for i in range(6)]
SWH = sum(SW)
NE = 8
EI = 512
EPS = 1e-5
EPS_F32 = float(np.finfo(np.float32).eps)
RSQRT_SEED = float(0x5F3759DF)
NEG = -1.0e30
PIECE_Q = (0, 0, 1, 1, 0, 2)
PIECE_K = (0, 1, 0, 1, 2, 0)
STG = 512

SEGMENTS = [("kg1", 2 * P), ("q", 2 * P), ("k", 2 * P), ("v", 2 * D), ("g", 2 * D), ("kg2", P), ("o", 2 * D),
            ("w1", 2 * SWH), ("w3", 2 * SWH), ("w2", 6 * D), ("qkv0", 2 * 768), ("qkv1", 2 * 768),
            ("wo0", 2 * D), ("wo1", 2 * D), ("wr", 2 * P)]
SEGMENTS += [(f"{w}{e}", 1024) for e in range(NE) for w in ("eg", "eu", "ed")]


def jobs():
    out, at = [], 0
    for name, n in SEGMENTS:
        for c in range(0, n, STG):
            m = min(STG, n - c)
            out.append((name, c, m, at + c))
        at += n
    return out


JOBS = jobs()
LAST_JOB = {name: i for i, (name, *_r) in enumerate(JOBS)}

CONST = [("ident", P), ("sel", 8 * P), ("selt", 15 * H), ("rope", TPC * 8), ("iota", 8), ("one", 2), ("mask", P)]


class Tally:

    def __init__(self, sem, order):
        self.sem, self.order, self.n = sem, order, 0

    def tick(self, key):
        self.n += 1
        known = self.order.setdefault(key, self.n)
        assert known == self.n, (key, known, self.n)
        return self.sem, 1

    def upto(self, key):
        return self.sem, self.order.get(key, 1)


def build(nc, orders, w_pack, t_pack, c_pack, vec_pack, bias_pack, x_in, out):
    from contextlib import ExitStack
    ctx = ExitStack()
    with ctx:
        tallies = {}

        def tally(name):
            tallies[name] = Tally(ctx.enter_context(nc.semaphore(name)), orders.setdefault(name, {}))
            return tallies[name]

        def sem(name):
            return ctx.enter_context(nc.semaphore(name))

        cursor = [(nc.sbuf_base + 31) // 32 * 32]
        limit = nc.sbuf_usable_end

        def at(name, shape, dt, offset):
            return nc.alloc_sbuf_tensor_at(name, [P, *shape], dt, offset=offset)

        def size(shape, dt):
            n = math.prod(shape) * (2 if dt == BF16 else 4)
            return (n + 31) // 32 * 32

        def sb(name, shape, dt):
            o = cursor[0]
            cursor[0] = o + size(shape, dt)
            assert cursor[0] <= limit, (name, cursor[0], limit)
            return at(name, shape, dt, o)

        ident = sb("ident", [P], F32)
        rope = sb("rope", [TPC, 8], F32)
        iota8 = sb("iota8", [8], F32)
        one = sb("one", [2], F32)
        maskf = sb("maskf", [P], F32)
        identb = sb("identb", [P], BF16)
        maskb = sb("maskb", [P], BF16)
        vec = sb("vec", [16], F32)
        bias = sb("bias", [1280], F32)
        X = sb("X", [NT, D], F32)
        XN = sb("XN", [NT, D], F32)
        XA = sb("XA", [NT, D], F32)
        XTh = sb("XTh", [KC, NC * CH], F32R)
        XTl = sb("XTl", [KC, NC * CH], F32R)
        x1_at = cursor[0]
        X1h = sb("X1h", [KC, NC * CH], F32R)
        X1l = sb("X1l", [KC, NC * CH], F32R)
        NSTG = 3
        stg = sb("stg", [NSTG, STG], F32)
        mlp_at = cursor[0]
        sg = sb("sg", [2, CH], F32)
        hm = sb("hm", [3, CH], F32)
        ah = sb("ah", [3, CH], F32R)
        al = sb("al", [3, CH], F32R)
        st6 = sb("st6", [TPC, 6], F32)
        mv = sb("mv", [TPC, 2], F32)
        small = sb("small", [12, 64], F32)
        cw = sb("cw", [NT, 8], F32)
        m8 = sb("m8", [TPC, 8], F32)
        i8 = sb("i8", [TPC, 8], U32)
        region = cursor[0]

        def plan(items, start):
            o, made = start, {}
            for name, shape, dt in items:
                made[name] = at(name, shape, dt, o)
                o += size(shape, dt)
                assert o <= limit, (name, o, limit)
            return made, o

        r0, o = plan([("VTh", [2, NC * CH], F32R), ("VTl", [2, NC * CH], F32R), ("U", [3, CH], F32),
                      ("S", [2, CH], F32), ("QS", [2, CH], F32)], region)
        ffw_at = o
        m0, o = plan([("wgu", [KC, 2048], F32R), ("wpr", [8, D], F32R)], o)
        m1, _ = plan([("w1h", [2, SWH], F32R), ("w1l", [2, SWH], F32R), ("w3h", [2, SWH], F32R),
                      ("w3l", [2, SWH], F32R)], ffw_at)
        qka_at = o
        m2, o = plan([("QT", [NC * CH], F32), ("KT", [NC * CH], F32), ("AT", [NC * CH], F32)], o)
        m3, _ = plan([("w2h", [6, D], F32R), ("w2l", [6, D], F32R)], qka_at)
        names0 = []
        for n, c in (("kg1", 256), ("q", 256), ("k", 256), ("v", 512), ("kg2", 128), ("g", 512), ("o", 512)):
            names0 += [(n + "h", [c], F32R), (n + "l", [c], F32R)]
        proj_w_at = o
        o_w_at = proj_w_at + 15 * 1024
        m4, o = plan(names0 + [("sel", [8, P], F32R), ("selt", [15 * H], F32), ("KGh", [CH], F32R), ("KGl", [CH], F32R),
                      ("sq", [1, CH], F32), ("acc", [2, CH], F32)], o)
        m5, o1 = plan([("OT", [2, CH], F32), ("otok", [TPC, D], F32), ("cen", [TPC, D], F32)], proj_w_at)
        assert o1 <= o_w_at
        m6, o2 = plan([("wf", [2, CH], F32), ("wb", [CH], BF16), ("ab", [2, CH], BF16), ("sgn", [2, CH], BF16),
                       ("ms", [2, CH], BF16), ("wq", [2, CH], BF16)], o)
        L0 = {**r0, **m0, **m1, **m2, **m3, **m4, **m5, **m6}
        slot_at = [region + 32768, region]
        stacks = []
        for s in range(2):
            q, o = plan([(f"Qs{s}", [H, CH], BF16), (f"Ks{s}", [H, CH], BF16)], slot_at[s])
            stacks.append((q[f"Qs{s}"], q[f"Ks{s}"]))
        qkv_w, _ = plan([("qkv0h", [2 * 768], F32R), ("qkv0l", [2 * 768], F32R), ("qkv1h", [2 * 768], F32R),
                         ("qkv1l", [2 * 768], F32R)], slot_at[1])
        l1, o = plan([("Va0", [NT, H, 17], F32), ("Va1", [NT, H, 17], F32)], region + 65536)
        l1b, o1 = plan([("PTb", [4, 1280], F32), ("lgT", [CH], F32), ("lgs", [TPC, 8], F32), ("xan1", [TPC, D], F32),
                        ("Osb", [CH], F32), ("mtok", [TPC, 12], BF16), ("mT", [2, CH], BF16)], o)
        l1a, _ = plan([("P3", [2, 3, 4, CH], BF16)], o)
        l1c, o2 = plan([("qkt", [3, CH], F32), ("rr", [2, CH], F32), ("rt", [2, 32, 4], F32)], mlp_at)
        wo_w, _ = plan([("wo0h", [512], F32R), ("wo0l", [512], F32R), ("wo1h", [512], F32R), ("wo1l", [512], F32R),
                        ("wrh", [256], F32R), ("wrl", [256], F32R)], x1_at)
        pta, _ = plan([("PTa", [4, 1280], F32)], mlp_at)
        ew = []
        for s in range(2):
            q, _ = plan([(f"{w}{s}_{x}", [1024], F32R) for w in ("eg", "eu", "ed") for x in "hl"], slot_at[s])
            ew.append(q)
        L1 = {**l1, **l1a, **l1b, **l1c, **pta}
        CONSTS = 16 * (len(CONST) + 2)
        Wh, Wl = {}, {}
        for n in ("kg1", "q", "k", "v", "g", "kg2", "o"):
            Wh[n], Wl[n] = L0[n + "h"], L0[n + "l"]
        for n in ("w1", "w3", "w2"):
            Wh[n], Wl[n] = L0[n + "h"], L0[n + "l"]
        for n in ("qkv0", "qkv1"):
            Wh[n], Wl[n] = qkv_w[n + "h"], qkv_w[n + "l"]
        for n in ("wo0", "wo1", "wr"):
            Wh[n], Wl[n] = wo_w[n + "h"], wo_w[n + "l"]
        for e in range(NE):
            for w in ("eg", "eu", "ed"):
                Wh[f"{w}{e}"], Wl[f"{w}{e}"] = ew[e % 2][f"{w}{e % 2}_h"], ew[e % 2][f"{w}{e % 2}_l"]

        def flat(t):
            a = t[:]
            return a if len(a.shape) == 2 else a.rearrange("p a b -> p (a b)")

        def wv(t, n):
            return flat(t).rearrange("p (k n) -> p k n", n=n)

        banks = [ctx.enter_context(nc.psum_tensor(f"bank{i}", [P, CH], F32)) for i in range(8)]
        pieces = nc.dram_tensor("pieces", [4, 3, 512, CH], BF16).ap()

        s_const = sem("constants_loaded")
        s_x = [sem("x0_loaded"), sem("x1_loaded")]
        s_stg = [sem(f"stage{i}_loaded") for i in range(NSTG)]
        s_wf = [sem("ternary0_loaded"), sem("ternary1_loaded")]
        s_pw = [sem(f"pieces{n}_written") for n in range(4)]
        s_mrow = [sem("maxima_rows0_placed"), sem("maxima_rows1_placed")]
        s_stack = [[sem(f"stack{i}_half{j}_loaded") for j in range(2)] for i in range(2)]
        s_out = sem("output_written")
        dve_chain = tally("dve_chain")
        act_chain = tally("act_chain")
        pool_chain = tally("pool_chain")
        mm = tally("products_done")
        w_split = tally("weights_split")
        xn_ready = tally("normed_ready")
        hi = tally("high_parts")
        lo = tally("low_parts")
        proj = tally("projection_copied")
        dproj = tally("projection_taken")
        decay = tally("decay_ready")
        sgl = tally("silu_g_ready")
        t_abs = tally("ternary_abs")
        t_done = tally("ternary_weights")
        t_put = tally("ternary_stored")
        t_sgn = tally("ternary_signed")
        ug = tally("gla_update")
        sc = tally("gla_state")
        qs = tally("gla_readout")
        red = tally("gla_reduced")
        ot_copied = tally("gla_out_copied")
        g_sq = tally("group_squares")
        sgr = tally("gate_silu")
        hmr = tally("hidden_ready")
        ahr = tally("hidden_high")
        alr = tally("hidden_low")
        sqr = tally("hidden_square")
        accr = tally("square_sum")
        accr2 = tally("square_sum_dve")
        y = tally("mlp_out")
        ydone = tally("mlp_out_taken")
        tok = tally("token_rows")
        qk_act = tally("qk_rows_copied")
        rotated = tally("qk_rotated")
        p_h = tally("part_high")
        p_r = tally("part_rest")
        p_m = tally("part_mid")
        p_l = tally("part_low")
        v_ready = tally("v_rows")
        ones_set = tally("v_ones")
        mx = tally("row_max")
        mxp = tally("row_max_parts")
        mT_ready = tally("row_max_rows")
        ex = tally("probabilities")
        pv = tally("attention_sums")
        o_sb = tally("attention_copied")
        xbias = tally("out_bias_added")
        x_sum = tally("residual_summed")
        gate_e = tally("router_exp")
        setup = tally("constants_cast")

        units = [("ff", c) for c in range(NC)] + [("sw", c) for c in range(NC)]
        units += [(("moe", e), c) for e in range(NE) for c in range(NC)]
        steps, first = [], {}
        for u in units:
            first[u] = len(steps)
            n = FF_STEPS if u[0] == "ff" else 6 if u[0] == "sw" else EI // P
            steps += [(u, m, n) for m in range(n)]
        unit_no = {u: i for i, u in enumerate(units)}

        def steps_of(u):
            return [s for s in range(len(steps)) if steps[s][0] == u]

        FF = [s for c in range(NC) for s in steps_of(("ff", c))]
        SWS = [s for c in range(NC) for s in steps_of(("sw", c))]
        MOE = [s for u in units if u[0] not in ("ff", "sw") for s in steps_of(u)]
        LAG = 2
        PIECES = [0, 4, 8, 10, 1, 5, 2, 6, 9, 11, 3, 7]
        N_GLA = NC * H
        ff_slot = {4 + int(1.5 * s): s for s in FF}
        later = {11: [("ot", 0, 0)], 19: [("ot", 0, 1)], 35: [("ot", 1, 1)]}
        GN = [("otok", 0, 0), ("otok", 0, 1), ("gn", 0, 0), ("gn", 0, 1), ("gn", 0, 2), ("got", 0, 0), ("got", 0, 1),
              ("wo", 0, 0), ("wo", 0, 1), ("rms", 0, 0), ("xat", 0, 0), ("xat", 0, 1)]
        for x, at_ in zip(GN, [20, 21, 22, 25, 25, 26, 27, 28, 29, 31, 33, 34]):
            later.setdefault(at_, []).append(x)
        later.setdefault(27, []).append(("ot", 1, 0))

        def pieces_at(slot):
            return [(f"tern{stage}", PIECES[slot - stage]) for stage in (2, 1, 0) if 0 <= slot - stage < len(PIECES)]

        def pool_finishes(i):
            return i < 6

        def pool_sums(s):
            return s < 4

        def early(slot):
            return [("ternA", PIECES[slot])] + pieces_at(slot)

        T_AHEAD = 4
        ORDER = [("norm", 0, 0), ("norm", 0, 1), ("tr", 0), ("norm", 1, 0), ("norm", 1, 1), ("cast",), ("proj", 0), ("tr", 1),
                 ("z", 0)] + early(0) + [("e1", 0), ("proj", 1), ("sp", 0)] + early(1)
        ORDER += [("z", 1)] + early(2) + [("e1", 1)]
        for q_ in range(3, T_AHEAD):
            ORDER += early(q_)
        later[0] = [("sp", 1)]
        for c in range(NC):
            for pr in range(2):
                later[2 + 2 * c + pr] = [("silug", c, pr)]
        last_in = later_w = None
        for i in range(N_GLA + 4):
            p = pieces_at(i + T_AHEAD)
            ORDER += [("ternA", x[1]) for x in p if x[0] == "tern0"]
            for op, stage in (("scan", 2), ("read", 3), ("rep", 0), ("upd", 1)):
                if 0 <= i - stage < N_GLA:
                    ORDER.append((op, i - stage))
            if last_in is not None:
                ORDER.append(("hm", last_in))
                last_in = None
            ORDER += [x for x in p if x[0] == "tern1"]
            if 0 <= i - 4 < N_GLA:
                ORDER.append(("red", i - 4))
            ORDER += [x for x in p if x[0] != "tern1"]
            if i in ff_slot:
                last_in = ff_slot[i]
                ORDER.append(("in", last_in))
                if last_in >= LAG:
                    ORDER.append(("out", last_in - LAG))
                    if (last_in - LAG) % FF_STEPS == FF_STEPS - 1:
                        ORDER.append(("ss", (last_in - LAG) // FF_STEPS))
            if i - 1 in ff_slot and ff_slot[i - 1] == FF[-1]:
                ORDER += [("out", s) for s in FF[-LAG:]] + [("ss", NC - 1)]
                later_w = i + 1
            if later_w is not None:
                for k_ in (2 * (i - later_w), 2 * (i - later_w) + 1):
                    if 0 <= k_ < 6:
                        ORDER.append(("w", ("w1", "w3")[k_ // 3], k_ % 3))
            ORDER += later.get(i, [])
        W2 = [("w", "w2", k) for k in range(3)]
        ORDER += W2[:1]
        TAIL = [[("otok", 1, 0)], [("otok", 1, 1)], [("gn", 1, 0)], [("gn", 1, 1)], [("gn", 1, 2)], [("got", 1, 0)], [("got", 1, 1)],
                [("wo", 1, 0)], [("wo", 1, 1)], [("rms", 1, 0)], [("xat", 1, 0)], [("xat", 1, 1)],
                [("ln", 0, 1)], [("l1", 0, "xt", 0), ("l1", 0, "xt", 1)]]
        TAIL_AT = [0, 0, 0, 2, 4, 4, 4, 4, 4, 4, 5, 5, 9, 10]
        for i, s in enumerate(SWS):
            ORDER.append(("in", s))
            if i >= 1:
                ORDER.append(("hm", SWS[i - 1]))
            for x, at_ in zip(TAIL, TAIL_AT):
                if at_ == i:
                    ORDER += x
            if i == 0:
                ORDER += W2[1:]
            if i >= LAG:
                ORDER.append(("out", SWS[i - LAG]))
            if i == 8:
                ORDER += [("swout", 0), ("ln", 0, 0)]
            ORDER += [("qkvw", i)]
        ORDER += [("hm", SWS[-1])] + [("l1", 0, "x1", 0), ("l1", 0, "x1", 1)] + [("out", s) for s in SWS[-LAG:]]
        NORM_1 = [("ln", 1, 0), ("ln", 1, 1), ("l1", 1, "xt", 0), ("l1", 1, "xt", 1), ("l1", 1, "x1", 0), ("l1", 1, "x1", 1)]
        beside = {}
        for x, at_ in zip(NORM_1, [1, 3, 5, 5, 6, 7]):
            beside.setdefault(at_, []).append(x)
        N_TILES = 2 * NT
        ORDER += [("xb", 0), ("ones", 0), ("swout", 1)]
        for u in range(N_TILES + 3):
            if u < N_TILES:
                ORDER.append(("qk", u))
            if 0 <= u - 2 < N_TILES:
                ORDER.append(("feat", u - 2))
            if 0 <= u - 3 < N_TILES:
                ORDER.append(("mid", u - 3))
            ORDER += beside.get(u, [])
        ORDER += [("xb", 1), ("ones", 1), ("w", "wo0"), ("w", "wo1"), ("w", "wr"), ("ones", 2)]
        ST_LAG = 8
        N_HEADS = 4 * H
        QUADS = N_HEADS // 4
        CHAIN_AT = [0, 1, 2, 3, 4, 5, 6, 7, 8, 9, 10, 12, 12, 13]
        after = {}
        for n in range(4):
            c, a = n // 2, n % 2
            at0 = H * n + 21
            chain = [("at", n, 0), ("at", n, 1), ("wout", n, 0), ("wout", n, 1)]
            if a == 1:
                chain += [("xm", c, 0), ("xm", c, 1), ("xm", c, 2), ("xm", c, 3), ("mt", c, 0), ("mt", c, 1), ("lg", c),
                          ("lgt", c), ("rt", c, 0), ("rt", c, 1)]
            for x, at_ in zip(chain, CHAIN_AT):
                after.setdefault(at0 + at_, []).append(x)
        stack_at = {}
        for n in range(1, 4):
            for half in range(2):
                for j in range(6):
                    g = (6 * half + j) if n == 1 else H * (n - 1) + 8 * half + j
                    stack_at[g] = ("stk", n, half, j, g)
        for g in range(N_HEADS + ST_LAG):
            h_ = g - ST_LAG
            quad_end = g % 4 == 0 and 0 < g <= N_HEADS
            if quad_end:
                ORDER.append(("mxp", g // 4 - 1))
            if g < N_HEADS:
                ORDER.append(("s", g))
            if h_ > 4 and h_ % 4 != 0:
                q = h_ // 4 - 1
                ORDER += [("pv", q, j) for j in {1: (0,), 2: (1,), 3: (2, 3)}[h_ % 4]]
            if h_ >= 0:
                ORDER.append(("st", h_))
            if quad_end:
                ORDER.append(("mxq", g // 4 - 1))
            if 20 <= g < 20 + NSTG:
                ORDER.append(("ld", LAST_JOB["wr"] + 1 + g - 20))
            if g in stack_at:
                ORDER.append(stack_at[g])
            if h_ % 4 == 1 and h_ > 8:
                ORDER.append(("ott", h_ // 4 - 2))
            ORDER += after.get(h_, [])
            if h_ == 3 * H:
                ORDER += [("w", f"{w}0") for w in ("eg", "eu", "ed")]
        last = [x for k in sorted(after) if k >= N_HEADS for x in after[k]]
        beside = [[("ott", QUADS - 2)] + [("pv", QUADS - 1, j) for j in range(TPC)], [("ott", QUADS - 1)] + last[0:4],
                  last[4:6], last[6:10], last[10:]]
        moe_units = [u for u in units if u[0] not in ("ff", "sw")]
        done = 0
        for i, s in enumerate(MOE):
            if i == EI // P:
                ORDER += beside[-1]
            ORDER.append(("in", s))
            if i < EI // P:
                ORDER += beside[i]
            ORDER.append(("hm", s))
            if i >= LAG:
                ORDER.append(("out", s - LAG))
            e, k = divmod(i, 8)
            if e + 1 < NE and k >= 2:
                ORDER.append(("ew", e + 1, k - 2))
            if i > LAG and steps[s - LAG - 1][1] == steps[s - LAG - 1][2] - 1:
                ORDER.append(("moeout", moe_units[done]))
                done += 1
        ORDER += [("out", s) for s in MOE[-LAG:]] + [("moeout", u) for u in moe_units[done:]]

        def spare(c, i):
            return 3 if c == 0 else i

        def side(last, i):
            return 6 + i if last else 7

        def part3(u, part):
            return L1["P3"][:, u // TPC % 2, part, :, u % TPC * P:(u % TPC + 1) * P]

        def l1_bank(c, k):
            return 2 * c + k

        def mlp_banks(s):
            if steps[s][0][0] == "ff":
                return 4, 5, 6
            if steps[s][0][0] == "sw":
                return (4, 5, 6) if (s - SWS[0]) % 2 == 0 else (2, 3, 6)
            i = s - MOE[0]
            return i % 2, 2 + i % 2, 4 + 2 * (unit_no[steps[s][0]] % 2)

        block = ctx.enter_context(nc.Block())

        def stack(sp, n, half, j):
            h0, h1 = 8 * half, 8 * half + 8
            for dst, row, part in ((stacks[n % 2][0], 0, PIECE_Q[j]), (stacks[n % 2][1], 256, PIECE_K[j])):
                src = pieces[n, part, row + HD * h0:row + HD * h1, :].rearrange("(h r) t -> r h t", r=HD)
                sp.dma_start(dst[HD * j:HD * (j + 1), h0:h1, :], src).then_inc(s_stack[n % 2][half], 16)

        @block.sync
        def _(sp):
            sp.dma_start(X[:, 0:TPC, :], x_in[0].rearrange("(t p) d -> p t d", p=P)).then_inc(s_x[0], 16)
            o = 0
            for (name, n), t in zip(CONST, (ident, L0["wf"], L0["selt"], rope, iota8, one, maskf)):
                src = c_pack[:, o:o + n]
                dst = flat(t)[:, 0:n]
                sp.dma_start(dst, src).then_inc(s_const, 16)
                o += n
            sp.dma_start(vec[:], vec_pack).then_inc(s_const, 16)
            sp.dma_start(bias[:], bias_pack).then_inc(s_const, 16)
            sp.dma_start(X[:, TPC:NT, :], x_in[1].rearrange("(t p) d -> p t d", p=P)).then_inc(s_x[1], 16)

            def load(j):
                if j >= NSTG:
                    sp.wait_ge(*w_split.upto(j - NSTG))
                _n, _c, m, src = JOBS[j]
                sp.dma_start(stg[:, j % NSTG, 0:m], w_pack[:, src:src + m]).then_inc(s_stg[j % NSTG], 16)

            n0 = LAST_JOB["o"] + 1
            for j in range(n0):
                load(j)
            sp.wait_ge(*setup.upto("sel"))
            for i, p in enumerate(PIECES):
                if i >= 2:
                    sp.wait_ge(*t_abs.upto((PIECES[i - 2], 0)))
                sp.dma_start(L0["wf"][:, i % 2, :], t_pack[:, p * CH:(p + 1) * CH]).then_inc(s_wf[i % 2], 16)
            for j in range(n0, LAST_JOB["qkv1"] + 1):
                load(j)
            def write_pieces(n):
                sp.wait_ge(*p_l.upto(4 * n + 3))
                for pc in range(3):
                    sp.dma_start(pieces[n, pc].rearrange("(b r) t -> r b t", r=P), L1["P3"][:, n % 2, pc]).then_inc(s_pw[n], 16)

            write_pieces(0)
            sp.wait_ge(s_pw[0], 48)
            for j in range(6):
                stack(sp, 0, 0, j)
            write_pieces(1)
            for j in range(6):
                stack(sp, 0, 1, j)
            write_pieces(2)
            write_pieces(3)
            sp.wait_ge(*mm.upto(("v", N_TILES // 2 - 1)))
            for j in range(LAST_JOB["qkv1"] + 1, LAST_JOB["wr"] + 1):
                load(j)
            for it in ORDER:
                if it[0] == "stk":
                    _, n, half, j, g = it
                    sp.wait_ge(*mm.upto(("s", g, 2)))
                    sp.wait_ge(s_pw[n], 48)
                    if n >= 2 and j == 0:
                        sp.wait_ge(*mm.upto(("st", H * (n - 2) + 8 * half + 7, 2)))
                    stack(sp, n, half, j)
                elif it[0] == "ld":
                    load(it[1])
                elif it[0] == "mxq":
                    q = it[1]
                    sp.wait_ge(*mT_ready.upto(q))
                    Q = stacks[q // 4 % 2][0]
                    for p_ in range(3):
                        h0 = q % 4 * 4
                        sp.dma_start(Q[96 + p_:97 + p_, h0:h0 + 4, :], L1["mT"][4 * p_:4 * p_ + 4, q % 2, :])\
                            .then_inc(s_mrow[q % 2], 16)
            for j in range(LAST_JOB["wr"] + 1 + NSTG, len(JOBS)):
                load(j)
            for c in range(NC):
                for pr in range(2):
                    for t in (2 * pr, 2 * pr + 1):
                        sp.wait_ge(*ydone.upto(((("moe", NE - 1), c), t)))
                    dst = out[c, 2 * pr * P:(2 * pr + 2) * P, :].rearrange("(t p) d -> p t d", p=P)
                    t0 = c * TPC + 2 * pr
                    sp.dma_start(dst, X[:, t0:t0 + 2, :]).then_inc(s_out, 16)
            sp.wait_ge(s_out, 4 * 16)

        @block.tensor
        def _(pe):
            held = {}

            def claim(b, who, key):
                if b in held:
                    pe.wait_ge(*held[b][0].upto(held[b][1]))
                held[b] = (who, key)

            def transposes(b, rows, n=TPC):
                for t in range(n):
                    last = nc.tensor.transpose(banks[b][:, t * P:(t + 1) * P], rows(t), ident[:])
                return last

            def product(outap, terms, start=True, stop=True, **kw):
                n = len(terms)
                for i, (a, b_) in enumerate(terms):
                    last = nc.tensor.matmul(outap, a, b_, start=start and i == 0, stop=stop and i == n - 1, **kw)
                return last

            def feature(b, w, n, col, M, xh, xl, c):
                h_, l_ = wv(Wh[w], n), wv(Wl[w], n)
                cs = slice(c * CH, (c + 1) * CH)
                terms = []
                for k in range(KC):
                    terms += [(h_[:, k, col:col + M], xh[:, k, cs]), (h_[:, k, col:col + M], xl[:, k, cs]),
                              (l_[:, k, col:col + M], xh[:, k, cs])]
                return product(banks[b][0:M, :], terms)

            def token(outap, w, n, col, N, xh, xl, t, **kw):
                h_, l_ = wv(Wh[w], n), wv(Wl[w], n)
                ts = slice(t * P, (t + 1) * P)
                terms = []
                for k in range(KC):
                    terms += [(xh[:, k, ts], h_[:, k, col:col + N]), (xh[:, k, ts], l_[:, k, col:col + N]),
                              (xl[:, k, ts], h_[:, k, col:col + N])]
                return product(outap, terms, **kw)

            def wait_w(name):
                pe.wait_ge(*w_split.upto(LAST_JOB[name]))

            pe.wait_ge(s_const, CONSTS)
            def rows_to_features(c):
                for v, src in (("x1", XA), ("xt", XN)):
                    pe.wait_ge(*xn_ready.upto((0, c, v)))
                    for k in range(KC):
                        b = (v == "x1") * 2 + k
                        key = (v, 0, c, k)
                        claim(b, lo, key)
                        transposes(b, lambda t: src[:, c * TPC + t, k * P:(k + 1) * P]).then_inc(*mm.tick(key))

            def project(c):
                for k in range(KC):
                    pe.wait_ge(*lo.upto(("x1", 0, c, k)))
                for b, (w, n, col, who, key) in enumerate([
                        ("kg1", P, 0, lo, ("kg", 0, c)), ("q", P, 0, proj, ("q", c)), ("k", P, 0, dproj, ("k", c)),
                        ("v", D, 0, lo, ("v", 0, c, 0)), ("v", D, P, lo, ("v", 0, c, 1))]):
                    wait_w(w)
                    claim(b, who, key)
                    feature(b, w, n, col, P, X1h, X1l, c).then_inc(*mm.tick(key))
                wait_w("g")
                for pr in range(2):
                    claim(5 + pr, dproj, ("g", c, pr))
                    for i in range(2):
                        last = token(banks[5 + pr][:, i * D:(i + 1) * D], "g", D, 0, D, X1h, X1l, c * TPC + 2 * pr + i)
                    last.then_inc(*mm.tick(("g", c, pr)))
                wait_w("kg2")
                pe.wait_ge(*lo.upto(("kg", 0, c)))
                claim(7, dproj, ("z", c))
                product(banks[7][:], [(Wh["kg2"][:], L0["KGh"][:]), (Wh["kg2"][:], L0["KGl"][:]),
                                      (Wl["kg2"][:], L0["KGh"][:])]).then_inc(*mm.tick(("z", c)))

            def to_products(p):
                pe.wait_ge(*t_sgn.upto(p))
                pe.wait_ge(*setup.upto("identb"))
                claim(3, t_put, p)
                bb = banks[3][:].bitcast(BF16)
                for q in range(4):
                    last = nc.tensor.transpose(bb[:, q * P:(q + 1) * P], L0["wq"][:, PIECES.index(p) % 2, q * P:(q + 1) * P],
                                               identb[:])
                last.then_inc(*mm.tick(("tern", p)))

            def mlp_in(s, gb, ub):
                (kind, c), m, n = steps[s]
                for b, gate, who in ((gb, True, sgr), (ub, False, hmr)):
                    claim(b, who, s)
                    key = ("gate" if gate else "up", s)
                    cs = slice(c * CH, (c + 1) * CH)
                    if kind == "ff":
                        if c == 0:
                            pe.wait_ge(*t_put.upto(m // 2 + (0 if gate else 4)))
                        col = (0 if gate else 1024) + m * P
                        terms = [(L0["wgu"][:, k, col:col + P], x[:, k, cs]) for k in range(KC) for x in (XTh, XTl)]
                        product(banks[b][:], terms).then_inc(*mm.tick(key))
                    elif kind == "sw":
                        feature(b, "w1" if gate else "w3", SWH, SWO[m], SW[m], X1h, X1l, c).then_inc(*mm.tick(key))
                    else:
                        feature(b, f"{'eg' if gate else 'eu'}{kind[1]}", EI, m * P, P, XTh, XTl, c).then_inc(*mm.tick(key))

            def mlp_out(s, yb):
                u, m, n = steps[s]
                kind, c = u
                pe.wait_ge(*alr.upto(s))
                if m == 0:
                    claim(yb, ydone, (u, 1))
                    claim(yb + 1, ydone, (u, 3))
                r = s % 3
                M = SW[m] if kind == "sw" else P
                if kind == "ff":
                    wh, wl = L0["wpr"][:, m, :], None
                    if c == 0:
                        for rt in range(2):
                            pe.wait_ge(*t_put.upto(8 + 2 * rt + m // 4))
                elif kind == "sw":
                    wh, wl = Wh["w2"][0:M, m, :], Wl["w2"][0:M, m, :]
                else:
                    wh, wl = (wv(W[f"ed{kind[1]}"], D)[:, m, :] for W in (Wh, Wl))
                    if m == 0 and c == 0:
                        wait_w(f"ed{kind[1]}")
                for t in range(TPC):
                    a_h, a_l = ah[0:M, r, t * P:(t + 1) * P], al[0:M, r, t * P:(t + 1) * P]
                    terms = [(a_h, wh), (a_l, wh)] + ([(a_h, wl)] if wl is not None else [])
                    last = product(banks[yb + t // 2][:, t % 2 * D:(t % 2 + 1) * D], terms,
                                   start=m == 0 and t % 2 == 0, stop=m == n - 1, skip_group_check=True)
                last.then_inc(*y.tick(s))

            def square_sums(c):
                pe.wait_ge(*accr2.upto(FF_STEPS * (c + 1) - 1))
                claim(4, dproj, ("ss", c))
                for t in range(TPC):
                    last = nc.tensor.matmul(banks[4][:, t:t + 1], L0["acc"][:, c, t * P:(t + 1) * P], one[:, 0:1],
                                            start=t == 0, stop=True, skip_group_check=True)
                last.then_inc(*mm.tick(("ss", c)))

            def to_tokens(c, pr):
                pe.wait_ge(*ot_copied.upto((c, 1)))
                b = spare(c, pr)
                claim(b, dproj, ("otok", c, pr))
                for i in range(2):
                    t = 2 * pr + i
                    for k in range(2):
                        last = nc.tensor.transpose(banks[b][:, i * D + k * P:i * D + (k + 1) * P],
                                                   L0["OT"][:, k, t * P:(t + 1) * P], ident[:])
                last.then_inc(*mm.tick(("otok", c, pr)))

            def replicate(i):
                c, d = i // H, i % H
                if d == 0:
                    for h2 in range(2):
                        pe.wait_ge(*lo.upto(("v", 0, c, h2)))
                claim(d % 2, ug, i)
                cs = slice(c * CH, (c + 1) * CH)
                product(banks[d % 2][:], [(L0["sel"][:, d % 8, :], L0["VTh"][:, d // 8, cs]),
                                          (L0["sel"][:, d % 8, :], L0["VTl"][:, d // 8, cs])]).then_inc(*mm.tick(("rep", i)))

            def reduce(i):
                pe.wait_ge(*qs.upto(i))
                c, d = i // H, i % H
                half, dd = d // 8, d % 8
                if dd == 0:
                    claim(2, ot_copied, (c, half))
                o = (7 - dd) * H
                nc.tensor.matmul(banks[2][:], L0["selt"][:, o:o + P], L0["QS"][:, i % 2, :],
                                 start=dd == 0, stop=dd == 7).then_inc(*red.tick(i))

            def split_rows(v, c, k, src, b):
                pe.wait_ge(*tok.upto((v, c)))
                key = (v, 0, c, k)
                claim(b, lo, key)
                transposes(b, lambda t: src[:, t, k * P:(k + 1) * P]).then_inc(*mm.tick(key))

            def tile(u):
                n = u // TPC
                return n % 2, n // 2, n // 2 * TPC + u % TPC

            def qk_project(u):
                a, c, t = tile(u)
                xh, xl = ((XTh, XTl), (X1h, X1l))[a]
                wait_w(f"qkv{a}")
                if u % TPC == 0:
                    for k in range(KC):
                        pe.wait_ge(*lo.upto((("xt", "x1")[a], 1, c, k)))
                claim(u % 2, dproj if a == 0 else qk_act, ("qkt", u))
                token(banks[u % 2][:], f"qkv{a}", 768, 0, 512, xh, xl, t).then_inc(*mm.tick(("qk", u)))
                b = 6 + u // 2 % 2
                if u % 2 == 0:
                    claim(b, v_ready, u // 2)
                last = token(banks[b][:, u % 2 * D:(u % 2 + 1) * D], f"qkv{a}", 768, 512, D, xh, xl, t)
                if u % 2 == 1:
                    last.then_inc(*mm.tick(("v", u // 2)))

            def to_feature(u):
                pe.wait_ge(*(rotated if tile(u)[0] == 0 else qk_act).upto(("qkt", u)))
                b = 4 + u % 2
                claim(b, p_r, u)
                transposes(b, lambda q: L1["qkt"][:, u % 3, q * P:(q + 1) * P]).then_inc(*mm.tick(("qkT", u)))

            S_GROUPS = [(2, (1,)), (1, (0, 2)), (0, (3,))]
            T_GROUPS = [(3, (0,)), (4, (1, 3)), (5, (2,))]

            def scores(g):
                n, h = g // H, g % H
                if h % 8 == 0:
                    pe.wait_ge(s_stack[n % 2][h // 8], 12 * 16 * (n // 2 + 1))
                Q, K = stacks[n % 2]
                for i_, (b, tiles) in enumerate(S_GROUPS):
                    claim(b, mx, (g, i_))
                    o = 0
                    for i in tiles:
                        w = (i + 1) * P
                        nc.tensor.matmul(banks[b][:, o:o + w], Q[0:96, h, i * P:(i + 1) * P], K[0:96, h, 0:w],
                                         start=True, stop=False)
                        last = nc.tensor.matmul(banks[b][:, o + w - P:o + w], identb[:], maskb[:], start=False, stop=True)
                        o += w
                    last.then_inc(*mm.tick(("s", g, i_)))

            def maxima_rows(q):
                pe.wait_ge(*mxp.upto(q))
                claim(7, mT_ready, q)
                bb = banks[7][:].bitcast(BF16)
                for t in range(TPC):
                    last = nc.tensor.transpose(bb[0:12, t * P:(t + 1) * P], L1["mtok"][:, t, :], identb[:])
                last.then_inc(*mm.tick(("mT", q)))

            def scores_t(g):
                n, h = g // H, g % H
                if h == 0:
                    pe.wait_ge(*ones_set.upto(n % 2))
                if h % 4 == 0:
                    pe.wait_ge(s_mrow[g // 4 % 2], 48 * (g // 8 + 1))
                Q, K = stacks[n % 2]
                for i_, (b, tiles) in enumerate(T_GROUPS):
                    claim(b, ex, (g, i_))
                    o = 0
                    for j in tiles:
                        w = (4 - j) * P
                        nc.tensor.matmul(banks[b][:, o:o + w], K[0:99, h, j * P:(j + 1) * P], Q[0:99, h, j * P:CH],
                                         start=True, stop=False)
                        last = nc.tensor.matmul(banks[b][:, o:o + P], maskb[:], identb[:], start=False, stop=True)
                        o += w
                    last.then_inc(*mm.tick(("st", g, i_)))

            PT_AT = [0, 512, 1024, 896]

            def attend(q, j):
                n = q // 4
                c, a = n // 2, n % 2
                if j == 0:
                    if q == 0:
                        pe.wait_ge(*ones_set.upto("v"))
                    for pr in range(2):
                        pe.wait_ge(*v_ready.upto(2 * n + pr))
                    for i_ in range(3):
                        pe.wait_ge(*ex.upto((4 * q + 3, i_)))
                    claim(6, o_sb, q)
                w = (4 - j) * P
                for hh in range(4):
                    pt = L1["PTa" if q % 2 == 0 else "PTb"]
                    last = nc.tensor.matmul(banks[6][32 * hh:32 * hh + 17, j * P:CH],
                                            L1[f"Va{a}"][:, c * TPC + j, 4 * (q % 4) + hh, :],
                                            pt[:, hh, PT_AT[j]:PT_AT[j] + w], start=j == 0, stop=j == 3,
                                            skip_group_check=True)
                if j == 3:
                    last.then_inc(*pv.tick(q))

            def attend_rows(q):
                pe.wait_ge(*o_sb.upto(q))
                claim(7, tok, ("att", q))
                transposes(7, lambda t: L1["Osb"][:, t * P:(t + 1) * P]).then_inc(*mm.tick(("ott", q)))

            for it in ORDER:
                op = it[0]
                if op == "tr":
                    rows_to_features(it[1])
                elif op == "proj":
                    project(it[1])
                elif op == "rep":
                    if it[1] == 0:
                        pe.wait_ge(*setup.upto("sel"))
                    replicate(it[1])
                elif op == "red":
                    reduce(it[1])
                elif op == "tern2":
                    to_products(it[1])
                elif op == "in":
                    if it[1] in SWS and steps[it[1]][1] == 0:
                        c = steps[it[1]][0][1]
                        for k in range(KC):
                            pe.wait_ge(*lo.upto(("xat", 0, c, k)))
                        for w in ("w1", "w3"):
                            wait_w(w)
                    if it[1] in MOE and steps[it[1]][1] == 0:
                        (_, e), c = steps[it[1]][0]
                        for k in range(KC):
                            pe.wait_ge(*lo.upto(("mt", 1, c, k)))
                        for w in ("eg", "eu"):
                            wait_w(f"{w}{e}")
                    if it[1] == MOE[0]:
                        pe.wait_ge(*o_sb.upto(QUADS - 2))
                    mlp_in(it[1], *mlp_banks(it[1])[0:2])
                elif op == "out":
                    if it[1] == SWS[0]:
                        wait_w("w2")
                    mlp_out(it[1], mlp_banks(it[1])[2])
                elif op == "ss":
                    square_sums(it[1])
                elif op == "otok":
                    to_tokens(it[1], it[2])
                elif op in ("got", "xat"):
                    split_rows(op, it[1], it[2], L0["cen"], spare(it[1], it[2]))
                elif op == "wo":
                    _, c, pr = it
                    wait_w("o")
                    for k in range(KC):
                        pe.wait_ge(*lo.upto(("got", 0, c, k)))
                    b = spare(c, pr)
                    claim(b, dproj, ("wo", c, pr))
                    for i in range(2):
                        last = token(banks[b][:, i * D:(i + 1) * D], "o", D, 0, D, X1h, X1l, c * TPC + 2 * pr + i)
                    last.then_inc(*mm.tick(("wo", c, pr)))
                elif op == "l1":
                    _, c, v, k = it
                    pe.wait_ge(*xn_ready.upto((1, c, v)))
                    b = l1_bank(c, k)
                    claim(b, lo, (v, 1, c, k))
                    src = XN if v == "xt" else XA
                    transposes(b, lambda t: src[:, c * TPC + t, k * P:(k + 1) * P]).then_inc(*mm.tick((v, 1, c, k)))
                elif op == "qk":
                    qk_project(it[1])
                elif op == "feat":
                    to_feature(it[1])
                elif op == "s":
                    scores(it[1])
                elif op == "mxq":
                    maxima_rows(it[1])
                elif op == "st":
                    scores_t(it[1])
                elif op == "pv":
                    attend(it[1], it[2])
                elif op == "ott":
                    attend_rows(it[1])
                elif op == "at":
                    _, n, k = it
                    pe.wait_ge(*tok.upto(("att", 4 * n + 3)))
                    claim(side(n == 3, k), lo, ("at", n, k))
                    transposes(side(n == 3, k), lambda t: XA[:, n // 2 * TPC + t, k * P:(k + 1) * P]).then_inc(*mm.tick(("at", n, k)))
                elif op == "wout":
                    _, n, pr = it
                    c, a = n // 2, n % 2
                    for k in range(KC):
                        pe.wait_ge(*lo.upto(("at", n, k)))
                    wait_w(f"wo{a}")
                    b = side(n == 3, pr)
                    claim(b, dproj, ("wout", n, pr))
                    for i in range(2):
                        last = token(banks[b][:, i * D:(i + 1) * D], f"wo{a}", D, 0, D, XTh, XTl, c * TPC + 2 * pr + i)
                    last.then_inc(*mm.tick(("wout", n, pr)))
                elif op == "mt":
                    _, c, k = it
                    pe.wait_ge(*tok.upto(("xm", c)))
                    claim(side(c == 1, k), lo, ("mt", 1, c, k))
                    transposes(side(c == 1, k), lambda t: L1["xan1"][:, t, k * P:(k + 1) * P]).then_inc(*mm.tick(("mt", 1, c, k)))
                elif op == "lg":
                    c = it[1]
                    for k in range(KC):
                        pe.wait_ge(*lo.upto(("mt", 1, c, k)))
                    wait_w("wr")
                    claim(7, proj, ("lg", c))
                    feature(7, "wr", P, 0, P, XTh, XTl, c).then_inc(*mm.tick(("lg", c)))
                elif op == "lgt":
                    c = it[1]
                    pe.wait_ge(*proj.upto(("lg", c)))
                    claim(7, dproj, ("lgt", c))
                    transposes(7, lambda t: L1["lgT"][:, t * P:(t + 1) * P]).then_inc(*mm.tick(("lgt", c)))

        @block.scalar
        def _(act):
            def link(ins):
                ins.then_inc(*act_chain.tick(act_chain.n))
                act.wait_ge(*act_chain.upto(act_chain.n - 1))

            def high(dst, b, key, scale=None, M=P):
                act.wait_ge(*mm.upto(key))
                src = banks[b][0:M, :]
                if scale is None:
                    ins = nc.scalar.copy(dst, src)
                else:
                    ins = nc.scalar.activation(dst, src, ACT.Copy, scale=scale)
                ins.then_inc(*hi.tick(key))

            act.wait_ge(s_const, CONSTS)
            def project(c):
                cs = slice(c * CH, (c + 1) * CH)
                if c == 1:
                    act.wait_ge(*mm.upto(("z", 0)))
                high(L0["KGh"][:], 0, ("kg", 0, c))
                act.wait_ge(*mm.upto(("q", c)))
                nc.scalar.copy(L0["QT"][:, cs], banks[1][:]).then_inc(*proj.tick(("q", c)))
                high(L0["VTh"][:, 0, cs], 3, ("v", 0, c, 0))
                high(L0["VTh"][:, 1, cs], 4, ("v", 0, c, 1))

            def put(i):
                act.wait_ge(*mm.upto(("tern", i)))
                src = banks[3][:].bitcast(BF16)[:, 0:CH]
                if i < 8:
                    dst = L0["wgu"][:, :, 2 * i * P:(2 * i + 2) * P].rearrange("p k (r n) -> p r k n", n=P)
                    src = src.rearrange("p (r k n) -> p r k n", r=2, k=2)
                else:
                    rt, q4 = (i - 8) // 2, (i - 8) % 2 * 4
                    dst = L0["wpr"][:, q4:q4 + 4, rt * P:(rt + 1) * P]
                    src = src.rearrange("p (k n) -> p k n", k=4)
                nc.scalar.copy(dst, src).then_inc(*t_put.tick(i))

            def absolute(p):
                i = PIECES.index(p)
                act.wait_ge(s_wf[i % 2], 16 * (i // 2 + 1))
                if i >= 2:
                    act.wait_ge(*t_sgn.upto(PIECES[i - 2]))
                link(nc.scalar.copy(L0["wb"][:], L0["wf"][:, i % 2, :]))
                nc.scalar.activation(L0["ab"][:, i % 2, :], L0["wb"][:], ACT.Abs).then_inc(*t_abs.tick((p, 0)))
                nc.scalar.activation(L0["sgn"][:, i % 2, :], L0["wb"][:], ACT.Sign).then_inc(*t_abs.tick((p, 1)))
                act.wait_ge(*t_abs.upto((p, 1)))

            def mlp_gate(s, gb):
                (kind, c), m, n = steps[s]
                M = SW[m] if kind == "sw" else P
                act.wait_ge(*mm.upto(("gate", s)))
                if s >= 2:
                    act.wait_ge(*hmr.upto(s - 2))
                nc.scalar.activation(sg[0:M, s % 2, :], banks[gb][0:M, :], ACT.Silu).then_inc(*sgr.tick(s))

            def mlp_high(s):
                (kind, c), m, n = steps[s]
                M = SW[m] if kind == "sw" else P
                act.wait_ge(*hmr.upto(s))
                if s >= 3:
                    act.wait_ge(*y.upto(s - 3))
                nc.scalar.copy(ah[0:M, s % 3, :], hm[0:M, s % 3, :]).then_inc(*ahr.tick(s))
                if kind == "ff":
                    if s >= 1:
                        act.wait_ge(*(accr if pool_sums(s - 1) else accr2).upto(s - 1))
                    nc.scalar.activation(L0["sq"][:, 0, :], hm[:, s % 3, :], ACT.Square).then_inc(*sqr.tick(s))

            def part_high(u):
                n = u // TPC
                act.wait_ge(*mm.upto(("qkT", u)))
                if u % TPC == 0 and n >= 2:
                    act.wait_ge(s_pw[n - 2], 48)
                nc.scalar.copy(part3(u, 0), banks[4 + u % 2][:].rearrange("p (b n) -> p b n", b=4)).then_inc(*p_h.tick(u))

            def part_mid(u):
                act.wait_ge(*p_r.upto(u))
                nc.scalar.copy(part3(u, 1), L1["rr"][:, u % 2, :].rearrange("p (b n) -> p b n", b=4)).then_inc(*p_m.tick(u))

            def qk_scaled(u):
                act.wait_ge(*mm.upto(("qk", u)))
                if u >= 3:
                    act.wait_ge(*mm.upto(("qkT", u - 3)))
                nc.scalar.activation(L1["qkt"][:, u % 3, 0:D], banks[u % 2][:, 0:D], ACT.Copy, scale=HD ** -0.5)\
                    .then_inc(*qk_act.tick(("q", u)))
                nc.scalar.copy(L1["qkt"][:, u % 3, D:2 * D], banks[u % 2][:, D:2 * D]).then_inc(*qk_act.tick(("qkt", u)))

            def exps(g):
                q = g // 4
                if g % 4 == 0:
                    if q >= 2:
                        act.wait_ge(*pv.upto(q - 2))
                    else:
                        act.wait_ge(*p_l.upto(N_TILES - 1))
                        for n in (2, 3):
                            act.wait_ge(s_pw[n], 48)
                pt = L1["PTa" if q % 2 == 0 else "PTb"]
                for i_, (b, lo_, w) in enumerate(((3, 0, 512), (4, 512, 512), (5, 1024, 256))):
                    act.wait_ge(*mm.upto(("st", g, i_)))
                    nc.scalar.activation(pt[:, g % 4, lo_:lo_ + w], banks[b][:, 0:w], ACT.Exp).then_inc(*ex.tick((g, i_)))

            for it in ORDER:
                op = it[0]
                if op == "tr":
                    c = it[1]
                    cs = slice(c * CH, (c + 1) * CH)
                    for k in range(KC):
                        high(X1h[:, k, cs], 2 + k, ("x1", 0, c, k), scale=vec[:, k:k + 1])
                    for k in range(KC):
                        high(XTh[:, k, cs], k, ("xt", 0, c, k))
                elif op == "proj":
                    project(it[1])
                elif op == "z":
                    act.wait_ge(*dproj.upto(("z", it[1])))
                    link(nc.scalar.activation(hm[:, 1, :], hm[:, 0, :], ACT.Abs))
                    nc.scalar.activation(hm[:, 1, :], hm[:, 1, :], ACT.Exp, scale=-1.0).then_inc(*decay.tick(("e", it[1])))
                elif op == "e1":
                    act.wait_ge(*dproj.upto(("e1", it[1])))
                    nc.scalar.activation(hm[:, 1, :], hm[:, 1, :], ACT.Ln).then_inc(*decay.tick(("ln", it[1])))
                elif op == "sp":
                    c = it[1]
                    act.wait_ge(*dproj.upto(("sp", c)))
                    nc.scalar.activation(L0["AT"][:, c * CH:(c + 1) * CH], hm[:, 1, :], ACT.Exp, scale=-1.0 / 16)\
                        .then_inc(*decay.tick(("a", c)))
                elif op == "silug":
                    _, c, pr = it
                    act.wait_ge(*dproj.upto(("g", c, pr)))
                    v = XA[:, c * TPC + 2 * pr:c * TPC + 2 * pr + 2, :]
                    nc.scalar.activation(v, v, ACT.Silu).then_inc(*sgl.tick((c, pr)))
                elif op == "ternA":
                    absolute(it[1])
                elif op == "tern2":
                    put(it[1])
                elif op == "in":
                    mlp_gate(it[1], mlp_banks(it[1])[0])
                elif op == "hm":
                    mlp_high(it[1])
                elif op == "ot":
                    _, c, half = it
                    act.wait_ge(*red.upto(c * H + 8 * half + 7))
                    if c == 1 and half == 0:
                        act.wait_ge(*mm.upto(("otok", 0, 1)))
                    nc.scalar.copy(L0["OT"][:, half, :], banks[2][:]).then_inc(*ot_copied.tick((c, half)))
                elif op == "gn" and it[2] == 0:
                    act.wait_ge(*tok.upto(("cen", it[1])))
                    nc.scalar.activation(flat(L0["otok"]), flat(L0["cen"]), ACT.Square).then_inc(*g_sq.tick(it[1]))
                elif op in ("got", "xat"):
                    _, c, k = it
                    high(X1h[:, k, c * CH:(c + 1) * CH], spare(c, k), (op, 0, c, k),
                         scale=None if op == "got" else vec[:, 2 + k:3 + k])
                elif op == "l1":
                    _, c, v, k = it
                    cs = slice(c * CH, (c + 1) * CH)
                    if v == "xt":
                        high(XTh[:, k, cs], l1_bank(c, k), (v, 1, c, k))
                    else:
                        high(X1h[:, k, cs], l1_bank(c, k), (v, 1, c, k), scale=vec[:, 4 + k:5 + k])
                elif op == "qk" and it[1] // TPC % 2 == 1:
                    qk_scaled(it[1])
                elif op == "feat":
                    part_high(it[1])
                elif op == "mid":
                    part_mid(it[1])
                elif op == "mxq":
                    q = it[1]
                    act.wait_ge(*mm.upto(("mT", q)))
                    if q >= 2:
                        act.wait_ge(s_mrow[q % 2], 48 * (q // 2))
                    nc.scalar.copy(L1["mT"][0:12, q % 2, :], banks[7][0:12, :].bitcast(BF16)[:, 0:CH]).then_inc(*mT_ready.tick(q))
                elif op == "st":
                    exps(it[1])
                elif op == "pv" and it[2] == 3:
                    q = it[1]
                    act.wait_ge(*pv.upto(q))
                    if q >= 1:
                        act.wait_ge(*mm.upto(("ott", q - 1)))
                    nc.scalar.copy(L1["Osb"][:], banks[6][:]).then_inc(*o_sb.tick(q))
                elif op == "at":
                    _, n, k = it
                    high(XTh[:, k, n // 2 * CH:(n // 2 + 1) * CH], side(n == 3, k), ("at", n, k))
                elif op == "mt":
                    _, c, k = it
                    high(XTh[:, k, c * CH:(c + 1) * CH], side(c == 1, k), ("mt", 1, c, k), scale=vec[:, 6 + k:7 + k])
                elif op == "lg":
                    act.wait_ge(*mm.upto(("lg", it[1])))
                    nc.scalar.copy(L1["lgT"][:], banks[7][:]).then_inc(*proj.tick(("lg", it[1])))
                elif op == "rt" and it[2] == 0:
                    act.wait_ge(*dproj.upto(("gap", it[1])))
                    nc.scalar.activation(small[:, 11, 0:TPC], small[:, 10, 0:TPC], ACT.Exp).then_inc(*gate_e.tick(it[1]))

        @block.vector
        def _(dve):
            def tell(ins):
                ins.then_inc(*dve_chain.tick(dve_chain.n))

            def told():
                dve.wait_ge(*dve_chain.upto(dve_chain.n - 1))

            def link(ins):
                tell(ins)
                told()

            def rsqrt_guess(y_, v, n, tmp):
                t_ = small[:, tmp, 0:n]
                link(nc.vector.tensor_single_scalar(t_.bitcast(I32), v.bitcast(I32), 1, ALU.logical_shift_right))
                link(nc.vector.tensor_scalar(y_.bitcast(I32), t_.bitcast(I32), -1.0, RSQRT_SEED, ALU.mult, ALU.add))

            def newton(y_, v, n, tmp, times):
                t_ = small[:, tmp, 0:n]
                for _ in range(times):
                    link(nc.vector.scalar_tensor_tensor(t_, y_, -0.5, v, ALU.mult, ALU.mult))
                    link(nc.vector.tensor_tensor(t_, t_, y_, ALU.mult))
                    link(nc.vector.scalar_tensor_tensor(y_, t_, 1.5, y_, ALU.add, ALU.mult))

            def rsqrt(y_, v, n, tmp):
                rsqrt_guess(y_, v, n, tmp)
                newton(y_, v, n, tmp, 3)

            def stats(src, c):
                for t in range(TPC):
                    tell(nc.vector.bn_stats(st6[:, t, :], src[:, c * TPC + t, :]))
                told()
                for t in range(TPC):
                    tell(nc.vector.bn_aggr(mv[:, t, :], st6[:, t, :]))
                told()

            def norm_stats(layer, c):
                stats(X, c)
                v, r = small[:, 0, 0:2 * TPC], small[:, 1, 0:2 * TPC]
                tell(nc.vector.tensor_scalar(v[:, 0:TPC], mv[:, :, 1], EPS, None, ALU.add))
                link(nc.vector.tensor_scalar(v[:, TPC:2 * TPC], mv[:, :, 1], 1.0 + EPS, EPS * EPS, ALU.mult, ALU.add))
                rsqrt(r, v, 2 * TPC, 4)

            def norm_rows(layer, c):
                r1, r2 = small[:, 1, 0:TPC], small[:, 1, TPC:2 * TPC]
                rows = [("xt", XN, r1), ("x1", XA, r2)]
                for v, dst, r in (rows if layer == 1 else rows[::-1]):
                    for t in range(TPC):
                        g = c * TPC + t
                        ins = nc.vector.tensor_scalar(dst[:, g, :], X[:, g, :], mv[:, t, 0:1], r[:, t:t + 1], ALU.subtract, ALU.mult)
                        if t < TPC - 1:
                            tell(ins)
                    ins.then_inc(*xn_ready.tick((layer, c, v)))
                for v in ("xt", "x1"):
                    dve.wait_ge(*xn_ready.upto((layer, c, v)))

            def low(dst, b, hi_t, key, scale=None):
                dve.wait_ge(*hi.upto(key))
                if scale is None:
                    ins = nc.vector.tensor_tensor(dst, banks[b][:], hi_t.bitcast(F32), ALU.subtract)
                else:
                    ins = nc.vector.scalar_tensor_tensor(dst, banks[b][:], scale, hi_t.bitcast(F32), ALU.mult, ALU.subtract)
                ins.then_inc(*lo.tick(key))

            def project(c):
                cs = slice(c * CH, (c + 1) * CH)
                low(L0["KGl"][:], 0, L0["KGh"][:], ("kg", 0, c))
                dve.wait_ge(*mm.upto(("k", c)))
                nc.vector.tensor_scalar(L0["KT"][:, cs], banks[2][:], HD ** -0.5, None, ALU.mult).then_inc(*dproj.tick(("k", c)))
                low(L0["VTl"][:, 0, cs], 3, L0["VTh"][:, 0, cs], ("v", 0, c, 0))
                low(L0["VTl"][:, 1, cs], 4, L0["VTh"][:, 1, cs], ("v", 0, c, 1))

            def gate_rows(c, pr):
                dve.wait_ge(*mm.upto(("g", c, pr)))
                t0 = c * TPC + 2 * pr
                nc.vector.tensor_tensor(XA[:, t0:t0 + 2, :], banks[5 + pr][:].rearrange("p (t d) -> p t d", t=2),
                                        bias[:, 0:D].unsqueeze(1).broadcast_to([P, 2, D]), ALU.add)\
                    .then_inc(*dproj.tick(("g", c, pr)))

            G = CH // 64

            def quantize(p):
                i = PIECES.index(p)
                scl, half, thr = small[:, 5, 0:G // 2].bitcast(BF16), small[:, 7, 0:G // 2].bitcast(BF16), small[:, 6, 0:G]
                ab, ms = L0["ab"][:, i % 2, :], L0["ms"][:, i % 2, :]
                g3 = lambda t: t.rearrange("p (g n) -> p g n", n=64)
                spread = lambda t: t.unsqueeze(2).broadcast_to([P, G, 64])
                dve.wait_ge(*t_abs.upto((p, 0)))
                link(nc.vector.tensor_reduce(thr, g3(ab), AX.X, ALU.add))
                tell(nc.vector.tensor_scalar(scl, thr, 1.0 / 64, 1e-8, ALU.mult, ALU.max))
                link(nc.vector.tensor_scalar(half, thr, 1.0 / 128, 0.5e-8, ALU.mult, ALU.max))
                if i >= 2:
                    dve.wait_ge(*t_sgn.upto(PIECES[i - 2]))
                link(nc.vector.tensor_tensor(g3(ms), g3(ab), spread(half), ALU.is_gt))
                if pool_finishes(i):
                    nc.vector.tensor_tensor(g3(ms), g3(ms), spread(scl), ALU.mult).then_inc(*t_done.tick(p))
                else:
                    link(nc.vector.tensor_tensor(g3(ms), g3(ms), spread(scl), ALU.mult))
                    link(nc.vector.tensor_tensor(ms, ms, ab, ALU.subtract))
                    nc.vector.tensor_tensor(ms, ab, ms, ALU.add).then_inc(*t_done.tick(p))
                dve.wait_ge(*t_done.upto(p))

            def mlp(s, ub):
                (kind, c), m, n = steps[s]
                M = SW[m] if kind == "sw" else P
                dve.wait_ge(*mm.upto(("up", s)))
                dve.wait_ge(*sgr.upto(s))
                if s == 0:
                    dve.wait_ge(*decay.upto(("a", NC - 1)))
                if s >= 3:
                    dve.wait_ge(*alr.upto(s - 3))
                    if steps[s - 3][0][0] == "ff":
                        dve.wait_ge(*sqr.upto(s - 3))
                nc.vector.tensor_tensor(hm[0:M, s % 3, :], sg[0:M, s % 2, :], banks[ub][0:M, :], ALU.mult).then_inc(*hmr.tick(s))

            def sum_squares(s):
                if s not in FF or pool_sums(s) or s in squares_summed:
                    return
                squares_summed.add(s)
                c = steps[s][0][1]
                dve.wait_ge(*sqr.upto(s))
                if steps[s][1] == 0:
                    ins = nc.vector.tensor_copy(L0["acc"][:, c, :], L0["sq"][:, 0, :])
                else:
                    dve.wait_ge(*(accr if pool_sums(s - 1) else accr2).upto(s - 1))
                    ins = nc.vector.tensor_tensor(L0["acc"][:, c, :], L0["acc"][:, c, :], L0["sq"][:, 0, :], ALU.add)
                ins.then_inc(*accr2.tick(s))

            squares_summed = set()

            def ff_out(c):
                u = ("ff", c)
                dve.wait_ge(*mm.upto(("ss", c)))
                v, r = small[:, 0, 0:TPC], small[:, 1, 0:TPC]
                nc.vector.tensor_scalar(v, banks[4][:, 0:TPC], 1.0 / 1024, EPS_F32, ALU.mult, ALU.add).then_inc(*dproj.tick(("ss", c)))
                dve.wait_ge(*dproj.upto(("ss", c)))
                rsqrt(r, v, TPC, 4)
                for t in range(TPC):
                    g = c * TPC + t
                    nc.vector.scalar_tensor_tensor(X[:, g, :], banks[6 + t // 2][:, t % 2 * D:(t % 2 + 1) * D], r[:, t:t + 1],
                                                   X[:, g, :], ALU.mult, ALU.add).then_inc(*ydone.tick((u, t)))

            def gla_update(i):
                c = i // H
                dve.wait_ge(*mm.upto(("rep", i)))
                if i % H == 0:
                    dve.wait_ge(*decay.upto(("a", c)))
                    dve.wait_ge(*dproj.upto(("k", c)))
                if i >= 3:
                    dve.wait_ge(*sc.upto(i - 3))
                nc.vector.tensor_tensor(L0["U"][:, i % 3, :], L0["KT"][:, c * CH:(c + 1) * CH], banks[i % 2][:], ALU.mult)\
                    .then_inc(*ug.tick(i))

            def gla_scan(i):
                c = i // H
                dve.wait_ge(*ug.upto(i))
                if i >= 2:
                    dve.wait_ge(*qs.upto(i - 2))
                nc.vector.tensor_tensor_scan(L0["S"][:, i % 2, :], L0["AT"][:, c * CH:(c + 1) * CH], L0["U"][:, i % 3, :], 0.0,
                                             ALU.mult, ALU.add).then_inc(*sc.tick(i))

            def rows_in(c, pr):
                dve.wait_ge(*mm.upto(("otok", c, pr)))
                nc.vector.tensor_copy(L0["otok"][:, 2 * pr:2 * pr + 2, :].rearrange("p t d -> p (t d)"),
                                      banks[spare(c, pr)][:]).then_inc(*dproj.tick(("otok", c, pr)))

            def group_norm(c, stage):
                sm, mn, vr, rs_ = (small[:, i, :] for i in (0, 1, 2, 8))
                byh = lambda t: t[:].rearrange("p t (d h) -> p t h d", h=H)
                nat = lambda t: t[:].rearrange("p t (d h) -> p t d h", h=H)
                wide = lambda s_: s_.rearrange("p (t h) -> p t h", h=H).unsqueeze(2).broadcast_to([P, TPC, HD, H])
                if stage == 0:
                    for pr in range(2):
                        dve.wait_ge(*dproj.upto(("otok", c, pr)))
                    if c == 1:
                        for k in range(KC):
                            dve.wait_ge(*mm.upto(("xat", 0, 0, k)))
                    link(nc.vector.tensor_reduce(sm.rearrange("p (t h) -> p t h", h=H), byh(L0["otok"]), AX.X, ALU.add))
                    link(nc.vector.tensor_scalar(mn, sm, 1.0 / HD, None, ALU.mult))
                    nc.vector.tensor_tensor(nat(L0["cen"]), nat(L0["otok"]), wide(mn), ALU.subtract)\
                        .then_inc(*tok.tick(("cen", c)))
                    dve.wait_ge(*tok.upto(("cen", c)))
                elif stage == 1:
                    dve.wait_ge(*g_sq.upto(c))
                    link(nc.vector.tensor_reduce(sm.rearrange("p (t h) -> p t h", h=H), byh(L0["otok"]), AX.X, ALU.add))
                    link(nc.vector.tensor_scalar(vr, sm, 1.0 / HD, EPS, ALU.mult, ALU.add))
                    rsqrt(rs_, vr, 64, 4)
                else:
                    link(nc.vector.tensor_tensor(nat(L0["cen"]), nat(L0["cen"]), wide(rs_), ALU.mult))
                    for pr in range(2):
                        dve.wait_ge(*sgl.upto((c, pr)))
                    nc.vector.tensor_tensor(L0["cen"][:], L0["cen"][:], XA[:, c * TPC:(c + 1) * TPC, :], ALU.mult)\
                        .then_inc(*tok.tick(("got", c)))

            def rms_factors(half):
                v, r = small[:, 0, 0:TPC], small[:, 1, 0:TPC]
                if half == 1:
                    link(nc.vector.tensor_tensor(v, mv[:, :, 0], mv[:, :, 0], ALU.mult))
                    link(nc.vector.scalar_tensor_tensor(v, v, EPS, mv[:, :, 1], ALU.add, ALU.add))
                    rsqrt_guess(r, v, TPC, 4)
                    newton(r, v, TPC, 4, 1)
                else:
                    newton(r, v, TPC, 4, 2)

            def rms_scale(c, dst, key):
                r = small[:, 1, 0:TPC]
                for t in range(TPC):
                    ins = nc.vector.tensor_scalar(dst[:, t, :], XA[:, c * TPC + t, :], r[:, t:t + 1], None, ALU.mult)
                    if t < TPC - 1:
                        tell(ins)
                ins.then_inc(*tok.tick((key, c)))

            def rms_rows(c, dst, key):
                stats(XA, c)
                rms_factors(1)
                rms_factors(2)
                rms_scale(c, dst, key)

            def sw_out(c):
                u = ("sw", c)
                for pr in range(2):
                    dve.wait_ge(*y.upto(steps_of(u)[-1]))
                    t0 = c * TPC + 2 * pr
                    link(nc.vector.tensor_tensor(XA[:, t0:t0 + 2, :], banks[6 + pr][:].rearrange("p (t d) -> p t d", t=2),
                                                 XA[:, t0:t0 + 2, :], ALU.add))
                    for i in range(2):
                        nc.vector.tensor_tensor(X[:, t0 + i, :], X[:, t0 + i, :], XA[:, t0 + i, :], ALU.add)\
                            .then_inc(*ydone.tick((u, 2 * pr + i)))
                dve.wait_ge(*ydone.upto((u, TPC - 1)))

            def part_rest(u):
                dve.wait_ge(*p_h.upto(u))
                b4 = lambda t_: t_.rearrange("p (b n) -> p b n", b=4)
                if u >= 2:
                    dve.wait_ge(*p_l.upto(u - 2))
                nc.vector.tensor_tensor(b4(L1["rr"][:, u % 2, :]), b4(banks[4 + u % 2][:]), part3(u, 0), ALU.subtract)\
                    .then_inc(*p_r.tick(u))

            def v_rows(u):
                n, pr = u // TPC, u // 2
                a, t0 = n % 2, n // 2 * TPC + u % TPC - 1
                dve.wait_ge(*mm.upto(("v", pr)))
                dst = L1[f"Va{a}"][:, t0:t0 + 2, :, 0:HD]
                src = banks[6 + pr % 2][:].rearrange("p (t h d) -> p t h d", t=2, h=H)
                if a == 0:
                    for i in range(2):
                        ins = nc.vector.tensor_tensor(dst[:, i], src[:, i],
                                                      bias[:, D + 512:D + 768].rearrange("p (h d) -> p h d", h=H), ALU.add)
                        if i == 0:
                            link(ins)
                else:
                    ins = nc.vector.tensor_copy(dst, src)
                ins.then_inc(*v_ready.tick(pr))

            def qk_rows(u):
                dve.wait_ge(*mm.upto(("qk", u)))
                if u >= 3:
                    dve.wait_ge(*mm.upto(("qkT", u - 3)))
                q = L1["qkt"][:, u % 3, :]
                nc.vector.tensor_tensor(q, banks[u % 2][:], bias[:, D:D + 512], ALU.add).then_inc(*dproj.tick(("qkt", u)))

            MX = small[:, 8, :]
            mxv = MX.rearrange("p (t h) -> p t h", h=H)

            def maxima(g):
                h = g % H
                for i_, (b, tiles) in enumerate([(2, (1,)), (1, (0, 2)), (0, (3,))]):
                    dve.wait_ge(*mm.upto(("s", g, i_)))
                    o = 0
                    for i in tiles:
                        w = (i + 1) * P
                        last = nc.vector.tensor_reduce(mxv[:, i, h:h + 1], banks[b][:, o:o + w], AX.X, ALU.max, negate=True)
                        o += w
                    last.then_inc(*mx.tick((g, i_)))

            def max_parts(q):
                dve.wait_ge(*mx.upto((4 * q + 3, 2)))
                if q >= 1:
                    dve.wait_ge(*mm.upto(("mT", q - 1)))
                mq = mxv[:, :, q % 4 * 4:q % 4 * 4 + 4]
                tv = lambda p_: L1["mtok"][:, :, p_ * 4:(p_ + 1) * 4]
                r = small[:, 9, 0:16].rearrange("p (t h) -> p t h", h=4)
                link(nc.vector.tensor_copy(tv(0), mq))
                link(nc.vector.tensor_tensor(r, mq, tv(0), ALU.subtract))
                link(nc.vector.tensor_copy(tv(1), r))
                nc.vector.tensor_tensor(tv(2), r, tv(1), ALU.subtract).then_inc(*mxp.tick(q))
                dve.wait_ge(*mxp.upto(q))

            def att_rows(q):
                c = q // 8
                dve.wait_ge(*mm.upto(("ott", q)))
                v = banks[7][:].rearrange("p (t h e) -> p t h e", t=TPC, h=4)
                rc = small[:, 7, 0:16].rearrange("p (t h) -> p t h", h=4)
                link(nc.vector.reciprocal(rc, v[:, :, :, HD]))
                if q % 4 == 0 and q // 4 % 2 == 1:
                    for k in range(KC):
                        dve.wait_ge(*mm.upto(("at", q // 4 - 1, k)))
                hs = 4 * (q % 4) * HD
                dst = XA[:, c * TPC:(c + 1) * TPC, hs:hs + 4 * HD].rearrange("p t (h d) -> p t h d", d=HD)
                nc.vector.tensor_tensor(dst, v[:, :, :, 0:HD], rc.unsqueeze(3).broadcast_to([P, TPC, 4, HD]), ALU.mult)\
                    .then_inc(*tok.tick(("att", q)))

            def out_rows(n, pr):
                c, a = n // 2, n % 2
                dve.wait_ge(*mm.upto(("wout", n, pr)))
                if a == 0:
                    dve.wait_ge(*xbias.upto(c))
                t0 = c * TPC + 2 * pr
                src = banks[side(n == 3, pr)][:].rearrange("p (t d) -> p t d", t=2)
                dst, add = ((X, X), (XA, XN))[a]
                nc.vector.tensor_tensor(dst[:, t0:t0 + 2, :], src, add[:, t0:t0 + 2, :], ALU.add)\
                    .then_inc(*dproj.tick(("wout", n, pr)))

            def router_top(c):
                dve.wait_ge(*mm.upto(("lgt", c)))
                nc.vector.tensor_copy(L1["lgs"][:], banks[7][:].rearrange("p (t n) -> p t n", n=P)[:, :, 0:8])\
                    .then_inc(*dproj.tick(("lgt", c)))
                dve.wait_ge(*dproj.upto(("lgt", c)))
                for t in range(TPC):
                    tell(nc.vector.max(m8[:, t, :], L1["lgs"][:, t, :]))
                told()

            def router_index(c):
                for t in range(TPC):
                    tell(nc.vector.max_index(i8[:, t, :], m8[:, t, :], L1["lgs"][:, t, :]))
                told()
                nc.vector.tensor_tensor(small[:, 10, 0:TPC], m8[:, :, 1], m8[:, :, 0], ALU.subtract).then_inc(*dproj.tick(("gap", c)))
                link(nc.vector.tensor_copy(small[:, 5, 0:2 * TPC].rearrange("p (t n) -> p t n", n=2), i8[:, :, 0:2]))

            def router_weights(c):
                idx = small[:, 5, 0:2 * TPC].rearrange("p (t n) -> p t n", n=2)
                dve.wait_ge(*gate_e.upto(c))
                e_, s_, p1, p2 = small[:, 11, 0:TPC], small[:, 0, 0:TPC], small[:, 1, 0:TPC], small[:, 2, 0:TPC]
                link(nc.vector.tensor_scalar(s_, e_, 1.0, None, ALU.add))
                link(nc.vector.reciprocal(p1, s_))
                link(nc.vector.tensor_tensor(p2, e_, p1, ALU.mult))
                w1_, w2_ = (small[:, i, 0:8 * TPC].rearrange("p (t e) -> p t e", e=8) for i in (3, 4))
                for t in range(TPC):
                    tell(nc.vector.tensor_scalar(w1_[:, t], iota8[:], idx[:, t, 0:1], p1[:, t:t + 1], ALU.is_equal, ALU.mult))
                    tell(nc.vector.tensor_scalar(w2_[:, t], iota8[:], idx[:, t, 1:2], p2[:, t:t + 1], ALU.is_equal, ALU.mult))
                told()
                link(nc.vector.tensor_tensor(cw[:, c * TPC:(c + 1) * TPC, :], w1_, w2_, ALU.add))

            def moe_out(u):
                (_, e), c = u
                dve.wait_ge(*y.upto(steps_of(u)[-1]))
                yb = 4 + 2 * (unit_no[u] % 2)
                if e >= 1:
                    dve.wait_ge(*ydone.upto(((("moe", e - 1), c), TPC - 1)))
                else:
                    dve.wait_ge(*x_sum.upto(c))
                for t in range(TPC):
                    g = c * TPC + t
                    nc.vector.scalar_tensor_tensor(X[:, g, :], banks[yb + t // 2][:, t % 2 * D:(t % 2 + 1) * D],
                                                   cw[:, g, e:e + 1], X[:, g, :], ALU.mult, ALU.add).then_inc(*ydone.tick((u, t)))

            for it in ORDER:
                op = it[0]
                if op == "norm":
                    _, c, stage = it
                    if stage == 0:
                        dve.wait_ge(s_x[c], 16)
                    (norm_stats if stage == 0 else norm_rows)(0, c)
                elif op == "cast":
                    nc.vector.tensor_copy(identb[:], ident[:]).then_inc(*setup.tick("identb"))
                    nc.vector.tensor_copy(maskb[:], maskf[:]).then_inc(*setup.tick("maskb"))
                    nc.vector.tensor_copy(flat(L0["sel"]), flat(L0["wf"])[:, 0:8 * P]).then_inc(*setup.tick("sel"))
                elif op == "tr":
                    c = it[1]
                    cs = slice(c * CH, (c + 1) * CH)
                    if c == 0:
                        dve.wait_ge(s_const, CONSTS)
                    for k in range(KC):
                        low(X1l[:, k, cs], 2 + k, X1h[:, k, cs], ("x1", 0, c, k), scale=vec[:, k:k + 1])
                    for k in range(KC):
                        low(XTl[:, k, cs], k, XTh[:, k, cs], ("xt", 0, c, k))
                elif op == "proj":
                    project(it[1])
                elif op == "z":
                    c = it[1]
                    dve.wait_ge(*mm.upto(("z", c)))
                    if c == 1:
                        dve.wait_ge(*decay.upto(("a", 0)))
                    nc.vector.tensor_scalar(hm[:, 0, :], banks[7][:], vec[:, 8:9], None, ALU.add).then_inc(*dproj.tick(("z", c)))
                    dve.wait_ge(*dproj.upto(("z", c)))
                    nc.vector.tensor_scalar(hm[:, 2, :], hm[:, 0, :], -1.0, 0.0, ALU.mult, ALU.max)\
                        .then_inc(*dproj.tick(("neg", c)))
                    gate_rows(c, 0)
                    gate_rows(c, 1)
                elif op == "e1":
                    dve.wait_ge(*decay.upto(("e", it[1])))
                    nc.vector.tensor_scalar(hm[:, 1, :], hm[:, 1, :], 1.0, None, ALU.add).then_inc(*dproj.tick(("e1", it[1])))
                elif op == "sp":
                    dve.wait_ge(*dproj.upto(("neg", it[1])))
                    dve.wait_ge(*decay.upto(("ln", it[1])))
                    nc.vector.tensor_tensor(hm[:, 1, :], hm[:, 1, :], hm[:, 2, :], ALU.add).then_inc(*dproj.tick(("sp", it[1])))
                elif op == "scan":
                    gla_scan(it[1])
                elif op == "upd":
                    gla_update(it[1])
                elif op == "tern0":
                    quantize(it[1])
                elif op == "hm":
                    mlp(it[1], mlp_banks(it[1])[1])
                    sum_squares(it[1] - 1)
                elif op == "ss":
                    sum_squares(FF_STEPS * (it[1] + 1) - 1)
                    ff_out(it[1])
                elif op == "otok":
                    if it[1] == 1:
                        dve.wait_ge(*g_sq.upto(0))
                    rows_in(it[1], it[2])
                elif op == "gn":
                    group_norm(it[1], it[2])
                elif op in ("got", "xat"):
                    _, c, k = it
                    cs = slice(c * CH, (c + 1) * CH)
                    low(X1l[:, k, cs], spare(c, k), X1h[:, k, cs], (op, 0, c, k),
                        scale=None if op == "got" else vec[:, 2 + k:3 + k])
                elif op == "wo":
                    _, c, pr = it
                    dve.wait_ge(*mm.upto(("wo", c, pr)))
                    t0 = c * TPC + 2 * pr
                    nc.vector.tensor_tensor(XA[:, t0:t0 + 2, :], banks[spare(c, pr)][:].rearrange("p (t d) -> p t d", t=2),
                                            XN[:, t0:t0 + 2, :], ALU.add).then_inc(*dproj.tick(("wo", c, pr)))
                elif op == "rms":
                    for pr in range(2):
                        dve.wait_ge(*dproj.upto(("wo", it[1], pr)))
                    rms_rows(it[1], L0["cen"], "xat")
                elif op == "swout":
                    sw_out(it[1])
                elif op == "ln":
                    (norm_stats if it[2] == 0 else norm_rows)(1, it[1])
                elif op == "l1":
                    _, c, v, k = it
                    cs = slice(c * CH, (c + 1) * CH)
                    if v == "xt":
                        low(XTl[:, k, cs], l1_bank(c, k), XTh[:, k, cs], (v, 1, c, k))
                    else:
                        low(X1l[:, k, cs], l1_bank(c, k), X1h[:, k, cs], (v, 1, c, k), scale=vec[:, 4 + k:5 + k])
                elif op == "qk":
                    if it[1] // TPC % 2 == 0:
                        qk_rows(it[1])
                    if it[1] % 2 == 1:
                        v_rows(it[1])
                elif op == "feat":
                    part_rest(it[1])
                elif op == "s":
                    maxima(it[1])
                elif op == "mxp":
                    max_parts(it[1])
                elif op == "ott":
                    att_rows(it[1])
                elif op == "at":
                    _, n, k = it
                    cs = slice(n // 2 * CH, (n // 2 + 1) * CH)
                    low(XTl[:, k, cs], side(n == 3, k), XTh[:, k, cs], ("at", n, k))
                elif op == "wout":
                    out_rows(it[1], it[2])
                elif op == "xm":
                    c = it[1]
                    if it[2] == 0:
                        for pr in range(2):
                            dve.wait_ge(*dproj.upto(("wout", 2 * c + 1, pr)))
                        stats(XA, c)
                    elif it[2] in (1, 2):
                        rms_factors(it[2])
                    else:
                        if c == 1:
                            for k in range(KC):
                                dve.wait_ge(*mm.upto(("mt", 1, 0, k)))
                        rms_scale(c, L1["xan1"], "xm")
                elif op == "mt":
                    _, c, k = it
                    cs = slice(c * CH, (c + 1) * CH)
                    low(XTl[:, k, cs], side(c == 1, k), XTh[:, k, cs], ("mt", 1, c, k), scale=vec[:, 6 + k:7 + k])
                elif op == "lgt":
                    router_top(it[1])
                elif op == "rt":
                    (router_index, router_weights)[it[2]](it[1])
                elif op == "moeout":
                    moe_out(it[1])

        @block.gpsimd
        def _(pool):
            def split_job(j):
                name, c, m, _src = JOBS[j]
                pool.wait_ge(s_stg[j % NSTG], 16 * (j // NSTG + 1))
                h_, l_ = flat(Wh[name])[:, c:c + m], flat(Wl[name])[:, c:c + m]
                src = stg[:, j % NSTG, 0:m]
                nc.gpsimd.tensor_scalar(h_, src, 1.0, 0.0, ALU.mult, ALU.add).then_inc(*pool_chain.tick(pool_chain.n))
                pool.wait_ge(*pool_chain.upto(pool_chain.n - 1))
                nc.gpsimd.tensor_tensor(l_, src, h_.bitcast(F32), ALU.subtract).then_inc(*w_split.tick(j))

            def seg(name):
                for j in range(len(JOBS)):
                    if JOBS[j][0] == name:
                        split_job(j)

            for n in ("kg1", "q", "k", "v", "g", "kg2", "o"):
                seg(n)
            def sign(p):
                i = PIECES.index(p)
                pool.wait_ge(*t_done.upto(p))
                pool.wait_ge(*t_abs.upto((p, 1)))
                if i >= 2:
                    pool.wait_ge(*mm.upto(("tern", PIECES[i - 2])))
                ms = L0["ms"][:, i % 2, :]
                if pool_finishes(i):
                    ab = L0["ab"][:, i % 2, :]
                    nc.gpsimd.tensor_tensor(ms, ms, ab, ALU.subtract).then_inc(*pool_chain.tick(pool_chain.n))
                    pool.wait_ge(*pool_chain.upto(pool_chain.n - 1))
                    nc.gpsimd.tensor_tensor(ms, ab, ms, ALU.add).then_inc(*pool_chain.tick(pool_chain.n))
                    pool.wait_ge(*pool_chain.upto(pool_chain.n - 1))
                nc.gpsimd.tensor_tensor(L0["wq"][:, i % 2, :], ms, L0["sgn"][:, i % 2, :], ALU.mult)\
                    .then_inc(*t_sgn.tick(p))

            def mlp(s):
                (kind, c), m, n = steps[s]
                M = SW[m] if kind == "sw" else P
                pool.wait_ge(*ahr.upto(s))
                nc.gpsimd.tensor_tensor(al[0:M, s % 3, :], hm[0:M, s % 3, :], ah[0:M, s % 3, :].bitcast(F32),
                                        ALU.subtract).then_inc(*alr.tick(s))
                if kind == "ff" and pool_sums(s):
                    pool.wait_ge(*sqr.upto(s))
                    if m == 0:
                        ins = nc.gpsimd.tensor_scalar(L0["acc"][:, c, :], L0["sq"][:, 0, :], 1.0, 0.0, ALU.mult, ALU.add)
                    else:
                        pool.wait_ge(*accr.upto(s - 1))
                        ins = nc.gpsimd.tensor_tensor(L0["acc"][:, c, :], L0["acc"][:, c, :], L0["sq"][:, 0, :], ALU.add)
                    ins.then_inc(*accr.tick(s))

            def read_out(i):
                c = i // H
                pool.wait_ge(*sc.upto(i))
                if i >= 2:
                    pool.wait_ge(*red.upto(i - 2))
                if i % H == 0:
                    pool.wait_ge(*proj.upto(("q", c)))
                nc.gpsimd.tensor_tensor(L0["QS"][:, i % 2, :], L0["QT"][:, c * CH:(c + 1) * CH], L0["S"][:, i % 2, :],
                                        ALU.mult).then_inc(*qs.tick(i))

            def rotate(u):
                pool.wait_ge(*dproj.upto(("qkt", u)))
                qv = L1["qkt"][:, u % 3, :].rearrange("p (h d) -> p h d", d=HD)
                wide = lambda lo_, n_: rope[:, u % TPC, lo_:lo_ + n_].unsqueeze(1).broadcast_to([P, 2 * H, n_])
                rt = L1["rt"]
                for dst, src, w in ((rt[:, 0], qv[:, :, 0:4], wide(0, 4)), (rt[:, 1, :, 0:2], qv[:, :, 2:4], wide(4, 2)),
                                    (rt[:, 1, :, 2:4], qv[:, :, 0:2], wide(6, 2))):
                    nc.gpsimd.tensor_tensor(dst, src, w, ALU.mult).then_inc(*pool_chain.tick(pool_chain.n))
                pool.wait_ge(*pool_chain.upto(pool_chain.n - 1))
                nc.gpsimd.tensor_tensor(qv[:, :, 0:4], rt[:, 0], rt[:, 1], ALU.add).then_inc(*rotated.tick(("qkt", u)))
                pool.wait_ge(*rotated.upto(("qkt", u)))

            qkv_jobs = [j for j in range(len(JOBS)) if JOBS[j][0] in ("qkv0", "qkv1")]
            for it in ORDER:
                op = it[0]
                if op == "tern1":
                    sign(it[1])
                elif op == "read":
                    read_out(it[1])
                elif op == "hm":
                    mlp(it[1])
                elif op == "w":
                    if it[1] == "w2":
                        pool.wait_ge(*red.upto(N_GLA - 1))
                    elif it[1] in ("w1", "w3"):
                        pool.wait_ge(*y.upto(FF[-1]))
                    elif it[1] in ("wo0", "wo1", "wr"):
                        pool.wait_ge(*mm.upto(("v", N_TILES // 2 - 1)))
                    else:
                        pool.wait_ge(*mm.upto(("st", 3 * H - 1, 2)))
                    if len(it) == 2:
                        seg(it[1])
                    else:
                        split_job([j for j in range(len(JOBS)) if JOBS[j][0] == it[1]][it[2]])
                elif op == "qkvw" and it[1] < len(qkv_jobs):
                    split_job(qkv_jobs[it[1]])
                elif op == "xb":
                    c = it[1]
                    pool.wait_ge(*xn_ready.upto((1, c, "xt")))
                    v = X[:, c * TPC:(c + 1) * TPC, :]
                    nc.gpsimd.tensor_tensor(v, v, bias[:, 1024:1280].unsqueeze(1).broadcast_to([P, TPC, D]), ALU.add)\
                        .then_inc(*xbias.tick(c))
                elif op == "ones":
                    if it[1] == 0:
                        pool.wait_ge(*y.upto(SWS[-1]))
                        for a in range(2):
                            nc.gpsimd.memset(L1[f"Va{a}"][:, :, :, HD:HD + 1], 1.0).then_inc(*ones_set.tick("v" if a else "v0"))
                        pool.wait_ge(*ones_set.upto("v"))
                    else:
                        pool.wait_ge(*mm.upto(("v", N_TILES // 2 - 1)))
                        pool.wait_ge(*xbias.upto(1))
                        pool.wait_ge(*p_l.upto(N_TILES - 1))
                        pool.wait_ge(*w_split.upto(LAST_JOB["qkv1" if it[1] == 1 else "wr"]))
                        slot = it[1] - 1
                        nc.gpsimd.memset(stacks[slot][1][96:99, :, :], 1.0).then_inc(*ones_set.tick(slot))
                        pool.wait_ge(*ones_set.upto(slot))
                elif op == "qk" and it[1] // TPC % 2 == 0:
                    rotate(it[1])
                elif op == "mid":
                    u = it[1]
                    pool.wait_ge(*p_m.upto(u))
                    nc.gpsimd.tensor_tensor(part3(u, 2), L1["rr"][:, u % 2, :].rearrange("p (b n) -> p b n", b=4), part3(u, 1),
                                            ALU.subtract).then_inc(*p_l.tick(u))
                elif op == "xm" and it[2] == 0:
                    c = it[1]
                    for n in (2 * c, 2 * c + 1):
                        for pr in range(2):
                            pool.wait_ge(*dproj.upto(("wout", n, pr)))
                    v = X[:, c * TPC:(c + 1) * TPC, :]
                    nc.gpsimd.tensor_tensor(v, v, XA[:, c * TPC:(c + 1) * TPC, :], ALU.add).then_inc(*x_sum.tick(c))
                elif op == "ew":
                    _, e, k = it
                    if k == 0:
                        pool.wait_ge(*(y.upto(MOE[(e - 1) * 8 - 1]) if e >= 2 else mm.upto(("st", N_HEADS - 1, 2))))
                    split_job([j for j in range(len(JOBS)) if JOBS[j][0] in (f"eg{e}", f"eu{e}", f"ed{e}")][k])


def pack_inputs(inp):
    f = {k: np.asarray(v) for k, v in inp.items()}

    def rows(w, n=None):
        K, N = w.shape
        kc = (K + P - 1) // P
        o = np.zeros((kc * P, n or N), w.dtype)
        o[:K, :N] = w
        return o.reshape(kc, P, -1).transpose(1, 0, 2).reshape(P, -1)

    by_value = lambda w: w.reshape(w.shape[0], H, HD).transpose(0, 2, 1).reshape(w.shape[0], D)
    seg = {"kg1": rows(f["L0_attn_Wkg1"], P), "q": rows(f["L0_attn_Wq"]), "k": rows(f["L0_attn_Wk"]),
           "v": rows(by_value(f["L0_attn_Wv"])), "g": rows(by_value(f["L0_attn_Wg"])), "kg2": rows(f["L0_attn_Wkg2"]),
           "o": rows(f["L0_attn_Wo"].reshape(H, HD, D).transpose(1, 0, 2).reshape(D, D)),
           "w1": rows(f["L0_attn_W1"]), "w3": rows(f["L0_attn_W3"])}
    w2 = np.zeros((6, P, D), np.float32)
    for i in range(6):
        w2[i, :SW[i]] = f["L0_attn_W2"][SWO[i]:SWO[i] + SW[i]]
    seg["w2"] = w2.transpose(1, 0, 2).reshape(P, -1)
    qkv = f["L1_attn_w_qkv"].reshape(D, H, 3, HD).transpose(0, 2, 1, 3).reshape(D, 768)
    seg["qkv0"] = rows(qkv)
    seg["qkv1"] = rows(np.concatenate([f["L1_ffn_Wq"].T, f["L1_ffn_Wk"].T, f["L1_ffn_Wv"].T], 1))
    seg["wo0"], seg["wo1"] = rows(f["L1_attn_w_out"]), rows(f["L1_ffn_Wo"].T)
    seg["wr"] = rows(f["L1_ffn_Wr"].T, P)
    for e in range(NE):
        seg[f"eg{e}"], seg[f"eu{e}"] = rows(f["L1_ffn_Wg"][e].T), rows(f["L1_ffn_Wu"][e].T)
        seg[f"ed{e}"] = rows(f["L1_ffn_Wd"][e].T)
    for name, n in SEGMENTS:
        assert seg[name].shape == (P, n), (name, seg[name].shape)
    w_pack = np.concatenate([seg[n] for n, _ in SEGMENTS], 1)
    gu = f["L0_ffn_w_gate_up"].reshape(16, P, D).transpose(1, 0, 2).reshape(P, -1)
    pr = f["L0_ffn_w_proj"].reshape(2, P, 1024).transpose(1, 0, 2).reshape(P, -1)
    t_pack = np.concatenate([gu, pr], 1)
    vec = np.zeros((P, 16), np.float32)
    for i, n in enumerate(("L0_attn_ln1_w", "L0_attn_ln2_w", "L1_ffn_w_ln1", "L1_ffn_w_ln2")):
        vec[:, 2 * i:2 * i + 2] = f[n].reshape(2, P).T
    vec[:, 8] = f["L0_attn_bkg2"]
    b = np.concatenate([f["L0_attn_bg"].reshape(H, HD).T.reshape(-1),
                        f["L1_attn_b_qkv"].reshape(H, 3, HD).transpose(1, 0, 2).reshape(-1), f["L1_attn_b_out"]])
    return w_pack, t_pack, vec, np.ascontiguousarray(np.broadcast_to(b, (P, 1280)))


def constants():
    ident = np.eye(P, dtype=np.float32)
    r = np.arange(P)
    sel = (r[:, None, None] == (np.arange(8)[None, :, None] * H + (r // KD)[None, None, :])).astype(np.float32)
    selt = np.zeros((P, 15 * H), np.float32)
    selt[r, 7 * H + r // KD] = 1
    pos = (np.arange(TPC)[None, :] * P + r[:, None]).astype(np.float32)
    inv = (1.0 / np.float32(10000.0) ** (np.arange(0, 4, 2, dtype=np.float32) / 4)).astype(np.float32)
    ang = (pos[:, :, None] * inv).astype(np.float32)
    co, si = np.cos(ang), np.sin(ang)
    rope = np.concatenate([co, co, -si, si], 2).astype(np.float32)
    iota = np.broadcast_to(np.arange(8, dtype=np.float32), (P, 8))
    parts = {"ident": ident, "sel": sel.reshape(P, -1), "selt": selt, "rope": rope.reshape(P, -1), "iota": iota,
             "one": np.ones((P, 2), np.float32), "mask": np.where(r[None, :] > r[:, None], NEG, 0.0)}
    c_pack = np.concatenate([parts[n] for n, _ in CONST], 1).astype(np.float32)
    return c_pack


def kernel(**inputs):
    import concourse.bacc as _bacc
    from concourse.bass_utils import run_bass_kernel_spmd as _run

    w_pack, t_pack, vec, bias = pack_inputs(inputs)
    c_pack = constants()
    arrays = {"w_pack": w_pack, "t_pack": t_pack, "c_pack": c_pack, "vec_pack": vec,
              "bias_pack": bias, "x_in": np.asarray(inputs["L0_attn_x"])}
    arrays = {k: np.ascontiguousarray(v) for k, v in arrays.items()}

    def program(orders):
        nc = _bacc.Bacc("TRN2", target_bir_lowering=False, num_devices=1)
        args = {k: nc.dram_tensor(k, list(v.shape), mybir.dt.from_np(v.dtype), kind="ExternalInput").ap()
                for k, v in arrays.items()}
        o = nc.dram_tensor("out", [NC, CH, D], F32, kind="ExternalOutput").ap()
        build(nc, orders, out=o, **args)
        return nc

    orders = {}
    program(orders)
    nc = program(orders)
    r = _run(nc, [arrays], core_ids=[0])
    return r.results[0]["out"]
```
